# Optimizing a Trainium2 kernel written in Bass

```python
import numpy as np
import jax
import jax.numpy as jnp

def _softmax(x, axis=-1):
    return jax.nn.softmax(x, axis=axis)

def _gelu(x):
    return jax.nn.gelu(x, approximate=True)

def _silu(x):
    return jax.nn.silu(x)

def _sigmoid(x):
    return jax.nn.sigmoid(x)

def _layernorm(x, axis=-1, eps=1e-05):
    m = jnp.mean(x, axis=axis, keepdims=True)
    v = jnp.var(x, axis=axis, keepdims=True)
    return (x - m) / jnp.sqrt(v + eps)

def _scatter_add(tgt, idx, src, axis=0):
    return tgt.at[idx].add(src)

def _segment_sum(src, seg, n):
    return jax.ops.segment_sum(src, seg, n)
kernel_name = 'mk_adj_seq_d1_adj_r2_938e06'

def setup_inputs(seed: int=0):
    np.random.seed(seed)
    _w = jnp.asarray

    def _rec_inputs():
        import jax
        import jax.numpy as jnp
        _gk = jax.random.key(seed)
        x = -0.000929 + 1 * jax.random.normal(jax.random.fold_in(_gk, 1), (4096, 128), jnp.float32)
        _w = (1.0 + jnp.arange(4096, dtype=jnp.float32)) ** (-0.5)
        _w = _w / _w.mean()
        _pij = jnp.clip(0.000976562 * _w[:, None] * _w[None, :], 0.0, 1.0)
        _a = jax.random.uniform(jax.random.fold_in(_gk, 2), (4096, 4096)) < _pij
        _a = jnp.logical_or(_a, jnp.eye(4096, dtype=bool))
        adj = _a.astype(jnp.int32)
        return (x, adj)
    x, adj = _rec_inputs()

    def _L0_gnn_setup():
        import jax, jax.numpy as jnp
        import numpy as np
        DIM = 128
        HEADS = 8
        DIM_FF = 512
        N = 2048
        HEAD_DIM = DIM // HEADS
        SCALE = HEAD_DIM ** (-0.5)

        def layer_norm(x, gamma, beta, eps=1e-05):
            mu = jnp.mean(x, axis=-1, keepdims=True)
            var = jnp.var(x, axis=-1, keepdims=True)
            return (x - mu) * jax.lax.rsqrt(var + eps) * gamma + beta
        key = jax.random.key(seed)
        ks = jax.random.split(key, 8)
        x = jax.random.normal(ks[0], (N, DIM), dtype=jnp.float32)
        adj = jax.random.randint(ks[1], (N, N), 0, 2, dtype=jnp.int32)
        adj = adj.at[jnp.arange(N), jnp.arange(N)].set(1)
        s = 1.0 / np.sqrt(DIM)
        w_qkv = jax.random.normal(ks[2], (DIM, 3 * DIM), dtype=jnp.float32) * s
        w_proj = jax.random.normal(ks[3], (DIM, DIM), dtype=jnp.float32) * s
        b_proj = jnp.zeros((DIM,), jnp.float32)
        w1 = jax.random.normal(ks[4], (DIM, DIM_FF), dtype=jnp.float32) * s
        b1 = jnp.zeros((DIM_FF,), jnp.float32)
        w2 = jax.random.normal(ks[5], (DIM_FF, DIM), dtype=jnp.float32) / np.sqrt(DIM_FF)
        b2 = jnp.zeros((DIM,), jnp.float32)
        g1 = jnp.ones((DIM,), jnp.float32)
        be1 = jnp.zeros((DIM,), jnp.float32)
        g2 = jnp.ones((DIM,), jnp.float32)
        be2 = jnp.zeros((DIM,), jnp.float32)
        return {'x': x, 'adj': adj, 'w_qkv': w_qkv, 'w_proj': w_proj, 'b_proj': b_proj, 'w1': w1, 'b1': b1, 'w2': w2, 'b2': b2, 'g1': g1, 'be1': be1, 'g2': g2, 'be2': be2}
    _L0_gnn_all = _L0_gnn_setup()
    _L0_gnn_in = {k: v for k, v in _L0_gnn_all.items() if k in ('w_qkv', 'w_proj', 'b_proj', 'w1', 'b1', 'w2', 'b2', 'g1', 'be1', 'g2', 'be2')}
    del _L0_gnn_all
    return {'x': x, 'adj': adj, 'L0_gnn_w_qkv': _L0_gnn_in['w_qkv'], 'L0_gnn_w_proj': _L0_gnn_in['w_proj'], 'L0_gnn_b_proj': _L0_gnn_in['b_proj'], 'L0_gnn_w1': _L0_gnn_in['w1'], 'L0_gnn_b1': _L0_gnn_in['b1'], 'L0_gnn_w2': _L0_gnn_in['w2'], 'L0_gnn_b2': _L0_gnn_in['b2'], 'L0_gnn_g1': _L0_gnn_in['g1'], 'L0_gnn_be1': _L0_gnn_in['be1'], 'L0_gnn_g2': _L0_gnn_in['g2'], 'L0_gnn_be2': _L0_gnn_in['be2']}

def reference(x, adj, L0_gnn_w_qkv, L0_gnn_w_proj, L0_gnn_b_proj, L0_gnn_w1, L0_gnn_b1, L0_gnn_w2, L0_gnn_b2, L0_gnn_g1, L0_gnn_be1, L0_gnn_g2, L0_gnn_be2):
    import jax
    import jax.numpy as jnp

    def _L0_gnn_ref(x, adj, w_qkv, w_proj, b_proj, w1, b1, w2, b2, g1, be1, g2, be2):
        import jax, jax.numpy as jnp
        import numpy as np
        DIM = 128
        HEADS = 8
        DIM_FF = 512
        N = 2048
        HEAD_DIM = DIM // HEADS
        SCALE = HEAD_DIM ** (-0.5)

        def layer_norm(x, gamma, beta, eps=1e-05):
            mu = jnp.mean(x, axis=-1, keepdims=True)
            var = jnp.var(x, axis=-1, keepdims=True)
            return (x - mu) * jax.lax.rsqrt(var + eps) * gamma + beta
        n = x.shape[0]
        qkv = layer_norm(x, g1, be1) @ w_qkv
        qkv = qkv.reshape(n, 3, HEADS, HEAD_DIM)
        q, k, v = (qkv[:, 0], qkv[:, 1], qkv[:, 2])
        scores = jnp.einsum('nhd,mhd->hnm', q, k) * SCALE
        mask = (adj != 0)[None, :, :]
        scores = jnp.where(mask, scores, -jnp.inf)
        attn = jax.nn.softmax(scores, axis=-1)
        out = jnp.einsum('hnm,mhd->nhd', attn, v).reshape(n, DIM)
        x = x + out @ w_proj + b_proj
        h2 = layer_norm(x, g2, be2)
        ff = jax.nn.gelu(h2 @ w1 + b1) @ w2 + b2
        return x + ff
    x = _L0_gnn_ref(x, adj, L0_gnn_w_qkv, L0_gnn_w_proj, L0_gnn_b_proj, L0_gnn_w1, L0_gnn_b1, L0_gnn_w2, L0_gnn_b2, L0_gnn_g1, L0_gnn_be1, L0_gnn_g2, L0_gnn_be2)
    return x

_drawn_inputs = setup_inputs


def setup_inputs(seed=0):
    import zlib

    import numpy as np

    out = dict(_drawn_inputs(seed))
    spreads = {'L0_gnn_b_proj': (0.0, 0.1),
     'L0_gnn_b1': (0.0, 0.1),
     'L0_gnn_b2': (0.0, 0.1),
     'L0_gnn_g1': (1.0, 0.2),
     'L0_gnn_be1': (0.0, 0.1),
     'L0_gnn_g2': (1.0, 0.2),
     'L0_gnn_be2': (0.0, 0.1)}
    factors = {}
    for name, (base, spread) in spreads.items():
        noise = np.random.default_rng([zlib.crc32(name.encode()), seed]).standard_normal(out[name].shape)
        drawn = base * np.exp(spread * noise) if base else spread * noise
        out[name] = jnp.asarray(drawn.astype(out[name].dtype))
    for name, factor in factors.items():
        out[name] = (out[name] * factor).astype(out[name].dtype)
    return out
```

```python
from contextlib import ExitStack

import concourse.bass as bass
from concourse import mybir

ALU = mybir.AluOpType
ACT = mybir.ActivationFunctionType
AX = mybir.AxisListType
F32 = mybir.dt.float32
I32 = mybir.dt.int32

P = 128
BANK = 512
HEADS = 8
EPS = 1e-5
MASKED = -1e30


def graph_layer(nc, x, adj, w_qkv, w_proj, b_proj, w1, b1, w2, b2, g1, be1, g2, be2, out):
    N, D = x.shape
    FF = w1.shape[1]
    HD = D // HEADS
    SCALE = float(HD) ** -0.5
    TILES = N // P
    GROUP = BANK // P
    GROUPS = TILES // GROUP
    CHUNKS = N // BANK
    FB = FF // P
    assert D == P and N % (2 * BANK) == 0 and FF == BANK

    qt_dram = nc.dram_tensor("q_transposed", (P, N), F32).ap()

    with ExitStack() as ctx:
        def sb(name, shape, dt=F32):
            return ctx.enter_context(nc.sbuf_tensor(name, shape, dt))

        def psum(name):
            return ctx.enter_context(nc.psum_tensor(name, [P, BANK], F32))

        def sem(name):
            return ctx.enter_context(nc.semaphore(name))

        w_qkv_sb = sb("w_qkv_sb", [P, 3 * D])
        w_proj_sb = sb("w_proj_sb", [P, D])
        w1_sb = sb("w1_sb", [P, FF])
        w2_sb = sb("w2_sb", [P, FB, D])
        norm_cols = sb("norm_cols", [P, 4])
        bias_rows = sb("bias_rows", [1, 2 * D + FF])
        ones_row = sb("ones_row", [1, P])
        eps_col = sb("eps_col", [P, 1])
        ident = sb("ident", [P, P])
        head_mask = sb("head_mask", [P, HEADS])

        keys_t = sb("keys_t", [P, N])
        values = sb("values", [P, TILES, D])

        x_grp = [sb(f"x_grp{b}", [P, GROUP, D]) for b in range(2)]
        stat6 = [sb(f"stat6_{b}", [P, GROUP, 6]) for b in range(2)]
        mean_var = [sb(f"mean_var{b}", [P, GROUP, 2]) for b in range(2)]
        std = [sb(f"std{b}", [P, GROUP]) for b in range(2)]
        rstd = [sb(f"rstd{b}", [P, GROUP]) for b in range(2)]
        h_t = [sb(f"h_t{b}", [P, BANK]) for b in range(2)]
        qt_stage = [sb(f"qt_stage{b}", [P, BANK]) for b in range(2)]

        adj_sb = sb("adj_sb", [P, N], I32)
        mask_bias = sb("mask_bias", [P, N])
        q_t = sb("q_t", [P, P])
        q_heads = sb("q_heads", [P, HEADS, P])
        scores = [sb(f"scores{b}", [P, N]) for b in range(2)]
        probs = sb("probs", [P, N])
        probs_t = sb("probs_t", [P, TILES, P])
        chunk_max = sb("chunk_max", [P, HEADS, CHUNKS])
        row_max = sb("row_max", [P, HEADS])
        neg_max = sb("neg_max", [P, HEADS])
        row_sum = sb("row_sum", [P, HEADS])
        inv_sum = sb("inv_sum", [P, HEADS])
        attn = sb("attn", [P, D])

        x_tile = sb("x_tile", [P, D])
        attn_t = sb("attn_t", [P, P])
        x2 = sb("x2", [P, D])
        e_stat6 = sb("e_stat6", [P, 6])
        e_mean_var = sb("e_mean_var", [P, 2])
        e_std = sb("e_std", [P, 1])
        e_rstd = sb("e_rstd", [P, 1])
        x2_norm = sb("x2_norm", [P, D])
        h2_t = sb("h2_t", [P, P])
        gelu = sb("gelu", [P, FF])
        y_tile = sb("y_tile", [P, D])

        ps_s = [psum("ps_s0"), psum("ps_s1")]
        ps_t = [psum("ps_t0"), psum("ps_t1")]
        ps_o = psum("ps_o")
        ps_e = [psum("ps_e0"), psum("ps_e1")]
        ps_x = psum("ps_x")

        weights_in = sem("weights_in")
        consts_made = sem("consts_made")
        ident_step = sem("ident_step")
        x_in = [sem("x_in0"), sem("x_in1")]
        p_stat6_made = sem("p_stat6_made")
        p_stats_made = sem("p_stats_made")
        p_std_made = sem("p_std_made")
        p_rstd_made = sem("p_rstd_made")
        p_norm_made = sem("p_norm_made")
        p_norm_turned = sem("p_norm_turned")
        p_h_made = sem("p_h_made")
        p_keys_ready = sem("p_keys_ready")
        p_queries_ready = sem("p_queries_ready")
        p_values_ready = sem("p_values_ready")
        p_keys_kept = sem("p_keys_kept")
        p_queries_kept = sem("p_queries_kept")
        p_values_kept = sem("p_values_kept")
        qt_stored = [sem("qt_stored0"), sem("qt_stored1")]
        adj_in = sem("adj_in")
        qt_in = sem("qt_in")
        bias_made = sem("bias_made")
        q_heads_made = sem("q_heads_made")
        scores_ready = sem("scores_ready")
        scores_masked = sem("scores_masked")
        row_max_made = sem("row_max_made")
        neg_max_made = sem("neg_max_made")
        probs_made = sem("probs_made")
        probs_turned = sem("probs_turned")
        turned_kept = [sem("turned_kept0"), sem("turned_kept1")]
        out_ready = sem("out_ready")
        inv_sum_made = sem("inv_sum_made")
        attn_made = sem("attn_made")
        xt_in = sem("xt_in")
        e_attn_turned = sem("e_attn_turned")
        e_attn_t_kept = sem("e_attn_t_kept")
        e_proj_ready = sem("e_proj_ready")
        e_x2_made = sem("e_x2_made")
        e_stat6_made = sem("e_stat6_made")
        e_stats_made = sem("e_stats_made")
        e_std_made = sem("e_std_made")
        e_rstd_made = sem("e_rstd_made")
        e_norm_made = sem("e_norm_made")
        e_norm_turned = sem("e_norm_turned")
        e_h2_made = sem("e_h2_made")
        e_ff1_ready = sem("e_ff1_ready")
        e_gelu_made = sem("e_gelu_made")
        e_ff2_ready = sem("e_ff2_ready")
        e_y_made = sem("e_y_made")
        y_stored = sem("y_stored")

        dve_past = sem("dve_past")

        WEIGHT_LOADS = 4 + 4 + 3

        block = ctx.enter_context(nc.Block())

        @block.sync
        def _(sp):
            sp.dma_start(w_qkv_sb[:], w_qkv).then_inc(weights_in, 16)
            sp.dma_start(w_proj_sb[:], w_proj).then_inc(weights_in, 16)
            sp.dma_start(w1_sb[:], w1).then_inc(weights_in, 16)
            sp.dma_start(w2_sb[:], w2.rearrange("(b p) d -> p b d", p=P)).then_inc(weights_in, 16)
            for i, v in enumerate((g1, be1, g2, be2)):
                sp.dma_start(norm_cols[:, i:i + 1], v.rearrange("(p a) -> p a", a=1)).then_inc(weights_in, 16)
            sp.dma_start(bias_rows[:, 0:D], b_proj.rearrange("(a d) -> a d", a=1)).then_inc(weights_in, 16)
            sp.dma_start(bias_rows[:, D:2 * D], b2.rearrange("(a d) -> a d", a=1)).then_inc(weights_in, 16)
            sp.dma_start(bias_rows[:, 2 * D:], b1.rearrange("(a d) -> a d", a=1)).then_inc(weights_in, 16)

            x_groups = x.rearrange("(g t p) d -> g p t d", t=GROUP, p=P)
            for b in range(2):
                sp.dma_start(x_grp[b][:], x_groups[b]).then_inc(x_in[b], 16)
            with sp.Fori(0, GROUPS // 2) as i:
                for b in range(2):
                    g = 2 * i + b
                    sp.wait_ge(p_queries_kept, g + 1)
                    sp.dma_start(qt_dram[:, bass.ds(g * BANK, BANK)], qt_stage[b][:]).then_inc(qt_stored[b], 16)
                    sp.wait_ge(p_norm_turned, g + 1)
                    nxt = sp.snap((g + 2) % GROUPS)
                    sp.dma_start(x_grp[b][:], x_groups[bass.ds(nxt, 1)].rearrange("a p t d -> p (a t) d")
                                 ).then_inc(x_in[b], 16)
            for b in range(2):
                sp.wait_ge(qt_stored[b], 16 * (GROUPS // 2))
                sp.wait_ge(x_in[b], 16 * (GROUPS // 2 + 1))

            x_tiles = x.rearrange("(t p) d -> p t d", p=P)
            adj_tiles = adj.rearrange("(t p) n -> p t n", p=P)
            out_tiles = out.rearrange("(t p) d -> p t d", p=P)

            def tile_loads(t, first):
                if not first:
                    sp.wait_ge(bias_made, t)
                sp.dma_start(adj_sb[:], adj_tiles[:, bass.ds(t, 1), :].rearrange("p a n -> p (a n)")).then_inc(adj_in, 16)
                if not first:
                    sp.wait_ge(q_heads_made, t)
                sp.dma_start(q_t[:], qt_dram[:, bass.ds(t * P, P)]).then_inc(qt_in, 16)
                if not first:
                    sp.wait_ge(e_x2_made, t)
                sp.dma_start(x_tile[:], x_tiles[:, bass.ds(t, 1), :].rearrange("p a n -> p (a n)")).then_inc(xt_in, 16)

            def tile_store(t):
                sp.wait_ge(e_y_made, t + 1)
                sp.dma_start(out_tiles[:, bass.ds(t, 1), :].rearrange("p a n -> p (a n)"), y_tile[:]).then_inc(y_stored, 16)

            tile_loads(0, True)
            with sp.Fori(1, TILES) as t:
                tile_loads(t, False)
                tile_store(t - 1)
            tile_store(TILES - 1)
            sp.wait_ge(y_stored, 16 * TILES)

        @block.gpsimd
        def _(pool):
            nc.gpsimd.memset(ident[:], 0.0).then_inc(ident_step, 1)
            nc.gpsimd.memset(head_mask[:], 1.0).then_inc(ident_step, 1)
            nc.gpsimd.memset(ones_row[:], 1.0).then_inc(consts_made, 1)
            nc.gpsimd.memset(eps_col[:], EPS).then_inc(consts_made, 1)
            pool.wait_ge(ident_step, 2)
            nc.gpsimd.affine_select(out=ident[:], in_=ident[:], compare_op=ALU.not_equal, fill=1.0, base=0,
                                    pattern=[[-1, P]], channel_multiplier=1).then_inc(consts_made, 1)
            nc.gpsimd.affine_select(out=head_mask[:], in_=head_mask[:], compare_op=ALU.is_ge, fill=0.0, base=0,
                                    pattern=[[-HD, HEADS]], channel_multiplier=1).then_inc(ident_step, 1)
            pool.wait_ge(ident_step, 3)
            nc.gpsimd.affine_select(out=head_mask[:], in_=head_mask[:], compare_op=ALU.is_ge, fill=0.0, base=HD - 1,
                                    pattern=[[HD, HEADS]], channel_multiplier=-1).then_inc(consts_made, 1)

        @block.tensor
        def _(pe):
            pe.wait_ge(consts_made, 4)
            pe.wait_ge(weights_in, 16 * WEIGHT_LOADS)

            def project_pair(i, first=False):
                for b in range(2):
                    g = 2 * i + b
                    pe.wait_ge(p_norm_made, g + 1)
                    for t in range(GROUP):
                        mm = nc.tensor.transpose(ps_s[b][:, t * P:(t + 1) * P], x_grp[b][:, t, :], ident[:])
                    mm.then_inc(p_norm_turned, 1)
                    pe.wait_ge(p_h_made, g + 1)
                    if not (first and b == 0):
                        pe.wait_ge(p_keys_kept, g)
                        pe.wait_ge(p_queries_kept, g)
                        pe.wait_ge(p_values_kept, g)
                    nc.tensor.matmul(ps_t[0][:], w_qkv_sb[:, D:2 * D], h_t[b][:], start=True, stop=True
                                     ).then_inc(p_keys_ready, 1)
                    nc.tensor.matmul(ps_t[1][:], w_qkv_sb[:, 0:D], h_t[b][:], start=True, stop=True
                                     ).then_inc(p_queries_ready, 1)
                    for t in range(GROUP):
                        mm = nc.tensor.matmul(ps_o[:, t * P:(t + 1) * P], h_t[b][:, t * P:(t + 1) * P],
                                              w_qkv_sb[:, 2 * D:3 * D], start=True, stop=True)
                    mm.then_inc(p_values_ready, 1)

            project_pair(0, True)
            with pe.Fori(1, GROUPS // 2) as i:
                project_pair(i)
            pe.wait_ge(p_keys_kept, GROUPS)
            pe.wait_ge(p_queries_kept, GROUPS)
            pe.wait_ge(p_values_kept, GROUPS)

            def head_scores(n, h, first):
                for c in range(CHUNKS):
                    k = (n * HEADS + h) * CHUNKS + c
                    if not (first and h == 0 and c < 2):
                        pe.wait_ge(scores_masked, k - 1)
                    nc.tensor.matmul(ps_s[c % 2][:], q_heads[:, h, :], keys_t[:, c * BANK:(c + 1) * BANK],
                                     start=True, stop=True).then_inc(scores_ready, 1)

            def head_turn(n, h, first):
                pe.wait_ge(probs_made, n * HEADS + h + 1)
                for j in range(TILES // GROUP):
                    k = (n * HEADS + h) * (TILES // GROUP) + j
                    if not (first and h == 0 and j < 2):
                        pe.wait_ge(turned_kept[j % 2], (n * HEADS + h) * (TILES // GROUP // 2) + j // 2)
                    for u in range(GROUP):
                        c = j * GROUP + u
                        mm = nc.tensor.transpose(ps_t[j % 2][:, u * P:(u + 1) * P], probs[:, c * P:(c + 1) * P], ident[:])
                    mm.then_inc(probs_turned, 1)

            def head_out(n, h, first):
                for j in range(2):
                    pe.wait_ge(turned_kept[j], (n * HEADS + h + 1) * (TILES // GROUP // 2))
                if h == 0 and not first:
                    pe.wait_ge(attn_made, n)
                for c in range(TILES):
                    mm = nc.tensor.matmul(ps_o[:, h * HD:(h + 1) * HD], probs_t[:, c, :],
                                          values[:, c, h * HD:(h + 1) * HD], start=(c == 0), stop=(c == TILES - 1))
                if h == HEADS - 1:
                    mm.then_inc(out_ready, 1)

            def tail(n):
                pe.wait_ge(attn_made, n + 1)
                nc.tensor.transpose(ps_e[0][:, 0:P], attn[:], ident[:]).then_inc(e_attn_turned, 1)
                pe.wait_ge(e_attn_t_kept, n + 1)
                nc.tensor.matmul(ps_e[1][:, 0:D], attn_t[:], w_proj_sb[:], start=True, stop=False)
                nc.tensor.matmul(ps_e[1][:, 0:D], ones_row[:], bias_rows[:, 0:D], start=False, stop=True
                                 ).then_inc(e_proj_ready, 1)
                pe.wait_ge(e_norm_made, n + 1)
                nc.tensor.transpose(ps_e[0][:, 0:P], x2_norm[:], ident[:]).then_inc(e_norm_turned, 1)
                pe.wait_ge(e_h2_made, n + 1)
                for f in range(FB):
                    nc.tensor.matmul(ps_e[1][:, f * P:(f + 1) * P], w1_sb[:, f * P:(f + 1) * P], h2_t[:],
                                     start=True, stop=False)
                    mm = nc.tensor.matmul(ps_e[1][:, f * P:(f + 1) * P],
                                          bias_rows[:, 2 * D + f * P:2 * D + (f + 1) * P], ones_row[:],
                                          start=False, stop=True)
                mm.then_inc(e_ff1_ready, 1)
                pe.wait_ge(e_gelu_made, n + 1)
                for f in range(FB):
                    nc.tensor.matmul(ps_e[0][:, 0:D], gelu[:, f * P:(f + 1) * P], w2_sb[:, f, :],
                                     start=(f == 0), stop=False)
                nc.tensor.matmul(ps_e[0][:, 0:D], ones_row[:], bias_rows[:, D:2 * D], start=False, stop=True
                                 ).then_inc(e_ff2_ready, 1)

            def dense_tile(n, first=False):
                pe.wait_ge(q_heads_made, n + 1)
                head_scores(n, 0, first)
                for h in range(HEADS):
                    if h + 1 < HEADS:
                        head_scores(n, h + 1, first)
                    head_turn(n, h, first)
                    head_out(n, h, first)
                tail(n)

            dense_tile(0, True)
            with pe.Fori(1, TILES) as n:
                dense_tile(n)

        @block.scalar
        def _(act):
            act.wait_ge(consts_made, 4)
            act.wait_ge(weights_in, 16 * WEIGHT_LOADS)
            with act.Fori(0, GROUPS // 2) as i:
                for b in range(2):
                    g = 2 * i + b
                    act.wait_ge(p_stats_made, g + 1)
                    nc.scalar.activation(std[b][:], mean_var[b][:, :, 1], ACT.Sqrt, bias=eps_col[:]
                                         ).then_inc(p_std_made, 1)
                    act.wait_ge(p_norm_turned, g + 1)
                    nc.scalar.activation(h_t[b][:], ps_s[b][:], ACT.Identity, bias=norm_cols[:, 1:2],
                                         scale=norm_cols[:, 0:1]).then_inc(p_h_made, 1)
                    act.wait_ge(p_keys_ready, g + 1)
                    nc.scalar.copy(keys_t[:, bass.ds(g * BANK, BANK)], ps_t[0][:]).then_inc(p_keys_kept, 1)

            def head_probs(n, h, first):
                act.wait_ge(neg_max_made, n * HEADS + h + 1)
                if not (first and h == 0):
                    act.wait_ge(probs_turned, (n * HEADS + h) * (TILES // GROUP))
                nc.scalar.activation(probs[:], scores[h % 2][:], ACT.Exp, bias=neg_max[:, h:h + 1], scale=SCALE,
                                     accum_out=row_sum[:, h:h + 1]).then_inc(probs_made, 1)
                for j in range(0, TILES // GROUP, 2):
                    act.wait_ge(probs_turned, (n * HEADS + h) * (TILES // GROUP) + j + 1)
                    nc.scalar.copy(probs_t[:, j * GROUP:(j + 1) * GROUP, :].rearrange("p a b -> p (a b)"), ps_t[0][:]
                                   ).then_inc(turned_kept[0], 1)

            def tail(n):
                act.wait_ge(e_attn_turned, n + 1)
                nc.scalar.copy(attn_t[:], ps_e[0][:, 0:P]).then_inc(e_attn_t_kept, 1)
                act.wait_ge(e_stats_made, n + 1)
                nc.scalar.activation(e_std[:], e_mean_var[:, 1:2], ACT.Sqrt, bias=eps_col[:]).then_inc(e_std_made, 1)
                act.wait_ge(e_norm_turned, n + 1)
                nc.scalar.activation(h2_t[:], ps_e[0][:, 0:P], ACT.Identity, bias=norm_cols[:, 3:4],
                                     scale=norm_cols[:, 2:3]).then_inc(e_h2_made, 1)
                act.wait_ge(e_ff1_ready, n + 1)
                nc.scalar.activation(gelu[:], ps_e[1][:], ACT.Gelu_apprx_tanh).then_inc(e_gelu_made, 1)

            def dense_tile(n, first=False):
                for h in range(HEADS):
                    head_probs(n, h, first)
                tail(n)

            dense_tile(0, True)
            with act.Fori(1, TILES) as n:
                dense_tile(n)

        @block.vector
        def _(dve):
            def project_pair(i, first=False):
                for b in range(2):
                    g = 2 * i + b
                    dve.wait_ge(x_in[b], 16 * (i + 1))
                    dve.sem_inc(dve_past, 1)
                    for t in range(GROUP):
                        ins = nc.vector.bn_stats(stat6[b][:, t, :], x_grp[b][:, t, :])
                    ins.then_inc(p_stat6_made, 1)
                    dve.wait_ge(p_stat6_made, g + 1)
                    dve.sem_inc(dve_past, 1)
                    for t in range(GROUP):
                        ins = nc.vector.bn_aggr(mean_var[b][:, t, :], stat6[b][:, t, :])
                    ins.then_inc(p_stats_made, 1)
                    dve.wait_ge(p_std_made, g + 1)
                    nc.vector.reciprocal(rstd[b][:], std[b][:]).then_inc(p_rstd_made, 1)
                    dve.wait_ge(p_rstd_made, g + 1)
                    for t in range(GROUP):
                        ins = nc.vector.tensor_scalar(x_grp[b][:, t, :], x_grp[b][:, t, :], mean_var[b][:, t, 0:1],
                                                      rstd[b][:, t:t + 1], ALU.subtract, ALU.mult)
                    ins.then_inc(p_norm_made, 1)
                    dve.wait_ge(p_queries_ready, g + 1)
                    if not first:
                        dve.wait_ge(qt_stored[b], 16 * i)
                    nc.vector.tensor_copy(qt_stage[b][:], ps_t[1][:]).then_inc(p_queries_kept, 1)
                    dve.wait_ge(p_values_ready, g + 1)
                    nc.vector.tensor_copy(values[:, bass.ds(g * GROUP, GROUP), :].rearrange("p a b -> p (a b)"), ps_o[:]
                                          ).then_inc(p_values_kept, 1)

            project_pair(0, True)
            with dve.Fori(1, GROUPS // 2) as i:
                project_pair(i)

            def head_mask_max(n, h, first):
                if not (first and h < 2):
                    dve.wait_ge(probs_made, n * HEADS + h - 1)
                for c in range(CHUNKS):
                    dve.wait_ge(scores_ready, (n * HEADS + h) * CHUNKS + c + 1)
                    dve.sem_inc(dve_past, 1)
                    nc.vector.tensor_tensor_reduce(
                        scores[h % 2][:, c * BANK:(c + 1) * BANK], ps_s[c % 2][:], mask_bias[:, c * BANK:(c + 1) * BANK],
                        1.0, MASKED, ALU.add, ALU.max, chunk_max[:, h, c:c + 1]).then_inc(scores_masked, 1)
                dve.wait_ge(scores_masked, (n * HEADS + h + 1) * CHUNKS)
                nc.vector.tensor_reduce(row_max[:, h:h + 1], chunk_max[:, h, :], AX.X, ALU.max).then_inc(row_max_made, 1)
                dve.wait_ge(row_max_made, n * HEADS + h + 1)
                nc.vector.tensor_scalar(neg_max[:, h:h + 1], row_max[:, h:h + 1], -SCALE, None, ALU.mult
                                        ).then_inc(neg_max_made, 1)

            def head_keep(n, h):
                for j in range(1, TILES // GROUP, 2):
                    dve.wait_ge(probs_turned, (n * HEADS + h) * (TILES // GROUP) + j + 1)
                    nc.vector.tensor_copy(probs_t[:, j * GROUP:(j + 1) * GROUP, :].rearrange("p a b -> p (a b)"),
                                          ps_t[1][:]).then_inc(turned_kept[1], 1)

            def tail(n):
                dve.wait_ge(xt_in, 16 * (n + 1))
                dve.wait_ge(e_proj_ready, n + 1)
                nc.vector.tensor_tensor(x2[:], ps_e[1][:, 0:D], x_tile[:], ALU.add).then_inc(e_x2_made, 1)
                dve.wait_ge(e_x2_made, n + 1)
                nc.vector.bn_stats(e_stat6[:], x2[:]).then_inc(e_stat6_made, 1)
                dve.wait_ge(e_stat6_made, n + 1)
                dve.sem_inc(dve_past, 1)
                nc.vector.bn_aggr(e_mean_var[:], e_stat6[:]).then_inc(e_stats_made, 1)
                dve.wait_ge(e_std_made, n + 1)
                nc.vector.reciprocal(e_rstd[:], e_std[:]).then_inc(e_rstd_made, 1)
                dve.wait_ge(e_rstd_made, n + 1)
                nc.vector.tensor_scalar(x2_norm[:], x2[:], e_mean_var[:, 0:1], e_rstd[:], ALU.subtract, ALU.mult
                                        ).then_inc(e_norm_made, 1)

            def tail_end(n, first):
                dve.wait_ge(e_ff2_ready, n + 1)
                if not first:
                    dve.wait_ge(y_stored, 16 * n)
                nc.vector.tensor_tensor(y_tile[:], ps_e[0][:, 0:D], x2[:], ALU.add).then_inc(e_y_made, 1)

            def dense_tile(n, first=False):
                dve.wait_ge(adj_in, 16 * (n + 1))
                nc.vector.tensor_scalar(mask_bias[:], adj_sb[:], 0.0, MASKED, ALU.is_equal, ALU.mult
                                        ).then_inc(bias_made, 1)
                dve.wait_ge(qt_in, 16 * (n + 1))
                for h in range(HEADS):
                    ins = nc.vector.tensor_scalar(q_heads[:, h, :], q_t[:], head_mask[:, h:h + 1], None, ALU.mult)
                ins.then_inc(q_heads_made, 1)
                dve.wait_ge(bias_made, n + 1)
                head_mask_max(n, 0, first)
                for h in range(HEADS):
                    if h + 1 < HEADS:
                        head_mask_max(n, h + 1, first)
                    head_keep(n, h)
                dve.wait_ge(probs_made, (n + 1) * HEADS)
                nc.vector.reciprocal(inv_sum[:], row_sum[:]).then_inc(inv_sum_made, 1)
                dve.wait_ge(inv_sum_made, n + 1)
                dve.wait_ge(out_ready, n + 1)
                nc.vector.tensor_tensor(attn[:].rearrange("p (h d) -> p h d", h=HEADS),
                                        ps_o[:, 0:D].rearrange("p (h d) -> p h d", h=HEADS),
                                        inv_sum[:].unsqueeze(2).broadcast_to([P, HEADS, HD]), ALU.mult
                                        ).then_inc(attn_made, 1)
                tail(n)
                tail_end(n, first)

            dve.wait_ge(consts_made, 4)
            dense_tile(0, True)
            with dve.Fori(1, TILES) as n:
                dense_tile(n)


NAMES = ["x", "adj"] + [f"L0_gnn_{n}" for n in
                        ("w_qkv", "w_proj", "b_proj", "w1", "b1", "w2", "b2", "g1", "be1", "g2", "be2")]


def kernel(**inputs):
    import numpy as np
    import concourse.bacc as bacc
    from concourse.bass_utils import run_bass_kernel_spmd

    nc = bacc.Bacc("TRN2", target_bir_lowering=False, num_devices=1)
    arrays, args = {}, []
    for name in NAMES:
        a = np.ascontiguousarray(inputs[name])
        arrays[f"in_{name}"] = a
        args.append(nc.dram_tensor(f"in_{name}", a.shape, mybir.dt.from_np(a.dtype), kind="ExternalInput").ap())
    out = nc.dram_tensor("out_0", inputs["x"].shape, F32, kind="ExternalOutput").ap()
    graph_layer(nc, *args, out)
    result = run_bass_kernel_spmd(nc, [arrays], core_ids=[0])
    return result.results[0]["out_0"]
```

```python
from contextlib import ExitStack

import concourse.bass as bass
from concourse import mybir

ALU = mybir.AluOpType
ACT = mybir.ActivationFunctionType
AX = mybir.AxisListType
F32 = mybir.dt.float32
BF16 = mybir.dt.bfloat16
I32 = mybir.dt.int32
U32 = mybir.dt.uint32

P = 128
BANK = 512
HEADS = 8
EPS = 1e-5
MASKED = -1e30
FAR = 1 << 20


class Kind:

    def __init__(self, chunks, slots):
        self.chunks, self.slots = chunks, slots
        self.rounds = -(-slots // 8)
        self.cands = 8 * chunks


def graph_layer(nc, x, adj, w_qkv, w_proj, b_proj, w1, b1, w2, b2, g1, be1, g2, be2, out):
    N, D = x.shape
    FF = w1.shape[1]
    HD = D // HEADS
    SCALE = float(HD) ** -0.5
    TILES = N // P
    GROUP = BANK // P
    GROUPS = TILES // GROUP
    CHUNKS = N // BANK
    FB = FF // P
    FOLDS = N // BANK
    assert D == P and FOLDS == 8 and FF == BANK

    SPARSE = TILES - 1
    WIDE, NARROW = Kind(8, 24), Kind(4, 16)
    EARLY = [WIDE, WIDE]
    MAX_SLOTS = 24
    RING_SLOTS = [max(k.slots for k in EARLY[b::2]) for b in range(2)]
    MAX_CANDS = 64

    def kind_of(s):
        return EARLY[s] if isinstance(s, int) and s < len(EARLY) else NARROW

    def gathers_until(s, b, r):
        if isinstance(s, int):
            return sum(kind_of(i).slots for i in range(b, s + 1, 2))
        return sum(k.slots for k in EARLY[b::2]) + NARROW.slots * (r + 1 - len(EARLY) // 2)

    kv_dram = nc.dram_tensor("keys_values", (N, 2 * D), F32).ap()
    q_dram = nc.dram_tensor("queries", (N, D), F32).ap()

    with ExitStack() as ctx:
        def sb(name, shape, dt=F32):
            return ctx.enter_context(nc.sbuf_tensor(name, shape, dt))

        def psum(name):
            return ctx.enter_context(nc.psum_tensor(name, [P, BANK], F32))

        def sem(name):
            return ctx.enter_context(nc.semaphore(name))

        w_qkv_sb = sb("w_qkv_sb", [P, 3 * D])
        w_proj_sb = sb("w_proj_sb", [P, D])
        w1_sb = sb("w1_sb", [P, FF])
        w2_sb = sb("w2_sb", [P, FB, D])
        norm_cols = sb("norm_cols", [P, 4])
        bias_rows = sb("bias_rows", [1, 2 * D + FF])
        ones_row = sb("ones_row", [1, P])
        ones_col = sb("ones_col", [P, 1])
        eps_col = sb("eps_col", [P, 1])
        ident = sb("ident", [P, P])
        head_mask = sb("head_mask", [P, HEADS])
        fold_weights = sb("fold_weights", [P, FOLDS, P], BF16)
        position = sb("position", [1, 2, BANK], BF16)
        ones_bf = sb("ones_bf", [1, P], BF16)
        fold_bit = sb("fold_bit", [P, FOLDS], I32)

        keys_t = sb("keys_t", [P, N])
        values = sb("values", [P, TILES, D])

        mask_bias = sb("mask_bias", [P, N], BF16)
        scores = sb("scores", [P, N])
        probs_t = sb("probs_t", [P, TILES, P])
        q_rows_d = sb("q_rows_d", [P, P])
        q_t = sb("q_t", [P, P])
        q_head = sb("q_head", [P, P])
        chunk_max = sb("chunk_max", [P, CHUNKS])
        row_max = sb("row_max", [P, 1])
        neg_max = sb("neg_max", [P, 1])
        row_sum = sb("row_sum", [P, 1])
        inv_sum_d = sb("inv_sum_d", [P, 1])
        attn_d = sb("attn_d", [P, D])

        def group_buf(whole, at, width):
            return whole[:, at * BANK:(at + width) * BANK]

        adj_landing = probs_t[:].rearrange("p a b -> p (a b)").bitcast(I32)
        probs_flat = probs_t[:].rearrange("p a b -> p (a b)")
        x_grp = [group_buf(scores, b, 1).rearrange("p (t d) -> p t d", t=GROUP) for b in range(2)]
        x_nrm = [group_buf(scores, 2 + b, 1).rearrange("p (t d) -> p t d", t=GROUP) for b in range(2)]
        h_t = [group_buf(scores, 4 + b, 1) for b in range(2)]
        q_stage = [group_buf(scores, 6 + b, 1) for b in range(2)]
        kv_stage = [group_buf(probs_flat, 2 * b, 2).rearrange("p (t d) -> p t d", t=GROUP) for b in range(2)]
        stat6 = [sb(f"stat6_{b}", [P, GROUP, 6]) for b in range(2)]
        mean_var = [sb(f"mean_var{b}", [P, GROUP, 2]) for b in range(2)]
        std = [sb(f"std{b}", [P, GROUP]) for b in range(2)]
        rstd = [sb(f"rstd{b}", [P, GROUP]) for b in range(2)]

        adj_sb = [sb(f"adj_sb{b}", [P, N], I32) for b in range(2)]
        nonzero = sb("nonzero", [P, N], BF16)
        cand = sb("cand", [P, MAX_CANDS])
        cand_int = sb("cand_int", [P, MAX_CANDS], I32)
        spread = sb("spread", [P, MAX_CANDS, FOLDS], I32)
        spread_rest = [sb(f"spread_rest{r}", [P, MAX_CANDS * FOLDS], I32) for r in range(2)]
        position_low, position_high = spread_rest[0][0:1, 0:BANK], spread_rest[1][0:1, 0:BANK]
        found = sb("found", [P, MAX_SLOTS])
        found_int = sb("found_int", [P, MAX_SLOTS], I32)
        low = sb("low", [P, MAX_SLOTS], I32)
        fold = sb("fold", [P, MAX_SLOTS], I32)
        column = sb("column", [P, MAX_SLOTS])
        slot_bias = [sb(f"slot_bias{b}", [P, MAX_SLOTS]) for b in range(2)]
        index = [sb(f"index{b}", [P, MAX_SLOTS], U32) for b in range(2)]
        worst_cand = sb("worst_cand", [P, 8])
        worst_found = sb("worst_found", [P, 1])
        worst = sb("worst", [P, 2])
        too_many = sb("too_many", [P, 1])
        dense_needed = sb("dense_needed", [1, 1], I32)

        gathered = [sb(f"gathered{b}", [P, RING_SLOTS[b], 2 * D]) for b in range(2)]
        q_tile = [sb(f"q_tile{b}", [P, D]) for b in range(2)]
        prod = sb("prod", [P, MAX_SLOTS, D])
        s_raw = sb("s_raw", [P, MAX_SLOTS, HEADS])
        s_msk = sb("s_msk", [P, MAX_SLOTS, HEADS])
        s_max = sb("s_max", [P, HEADS])
        s_sub = sb("s_sub", [P, MAX_SLOTS, HEADS])
        p_slot = sb("p_slot", [P, MAX_SLOTS, HEADS])
        p_sum = sb("p_sum", [P, HEADS])
        inv_sum = sb("inv_sum", [P, HEADS])
        attn = sb("attn", [P, D])

        x_tile = sb("x_tile", [P, D])
        attn_t = sb("attn_t", [P, P])
        x2 = sb("x2", [P, D])
        e_stat6 = sb("e_stat6", [P, 6])
        e_mean_var = sb("e_mean_var", [P, 2])
        e_std = sb("e_std", [P, 1])
        e_rstd = sb("e_rstd", [P, 1])
        x2_norm = sb("x2_norm", [P, D])
        h2_t = sb("h2_t", [P, P])
        gelu = sb("gelu", [P, FF])
        y_tile = sb("y_tile", [P, D])

        ps_s = [psum("ps_s0"), psum("ps_s1")]
        ps_t = [psum("ps_t0"), psum("ps_t1")]
        ps_o = psum("ps_o")
        ps_e = psum("ps_e")
        ps_c = psum("ps_c")
        ps_a = psum("ps_a")

        weights_in = sem("weights_in")
        consts_made = sem("consts_made")
        const_step = sem("const_step")
        dve_past = sem("dve_past")
        pool_past = sem("pool_past")
        x_in = [sem("x_in0"), sem("x_in1")]
        p_stat6_made = sem("p_stat6_made")
        p_stats_made = sem("p_stats_made")
        p_std_made = sem("p_std_made")
        p_rstd_made = sem("p_rstd_made")
        p_norm_made = sem("p_norm_made")
        p_norm_turned = sem("p_norm_turned")
        p_h_made = sem("p_h_made")
        p_kv_ready = [sem("p_kv_ready0"), sem("p_kv_ready1")]
        p_kv_kept = [sem("p_kv_kept0"), sem("p_kv_kept1")]
        p_q_ready = sem("p_q_ready")
        p_q_kept = sem("p_q_kept")
        p_keys_ready = sem("p_keys_ready")
        p_keys_kept = sem("p_keys_kept")
        p_values_kept = sem("p_values_kept")
        kv_stored = [sem("kv_stored0"), sem("kv_stored1")]
        q_stored = [sem("q_stored0"), sem("q_stored1")]
        adj_in = [sem("adj_in0"), sem("adj_in1")]
        squares_made = sem("squares_made")
        nonzero_made = sem("nonzero_made")
        codes_ready = sem("codes_ready")
        cands_found = sem("cands_found")
        cands_int = sem("cands_int")
        spread_made = sem("spread_made")
        round_found = sem("round_found")
        round_taken = sem("round_taken")
        found_read = sem("found_read")
        column_made = sem("column_made")
        index_made = sem("index_made")
        worst_step = sem("worst_step")
        kv_in = [sem("kv_in0"), sem("kv_in1")]
        index_read = sem("index_read")
        ring_clear = sem("ring_clear")
        q_in = [sem("q_in0"), sem("q_in1")]
        prod_made = sem("prod_made")
        s_raw_made = sem("s_raw_made")
        s_msk_made = sem("s_msk_made")
        s_max_made = sem("s_max_made")
        s_sub_made = sem("s_sub_made")
        p_made = sem("p_made")
        p_sum_made = sem("p_sum_made")
        weighted_made = sem("weighted_made")
        inv_sum_made = sem("inv_sum_made")
        sum_ready = sem("sum_ready")
        attn_made = sem("attn_made")
        d_adj_in = sem("d_adj_in")
        d_q_in = sem("d_q_in")
        d_bias_made = sem("d_bias_made")
        d_q_turned = sem("d_q_turned")
        d_q_kept = sem("d_q_kept")
        d_q_head = sem("d_q_head")
        d_scores_ready = sem("d_scores_ready")
        d_scores_masked = sem("d_scores_masked")
        d_row_max = sem("d_row_max")
        d_neg_max = sem("d_neg_max")
        d_probs_made = sem("d_probs_made")
        d_probs_turned = sem("d_probs_turned")
        d_turned_kept = [sem("d_turned_kept0"), sem("d_turned_kept1")]
        d_out_ready = sem("d_out_ready")
        d_inv_sum = sem("d_inv_sum")
        d_attn_made = sem("d_attn_made")
        xt_in = sem("xt_in")
        e_attn_turned = sem("e_attn_turned")
        e_attn_t_kept = sem("e_attn_t_kept")
        e_proj_ready = sem("e_proj_ready")
        e_x2_made = sem("e_x2_made")
        e_stat6_made = sem("e_stat6_made")
        e_stats_made = sem("e_stats_made")
        e_std_made = sem("e_std_made")
        e_rstd_made = sem("e_rstd_made")
        e_norm_made = sem("e_norm_made")
        e_norm_turned = sem("e_norm_turned")
        e_h2_made = sem("e_h2_made")
        e_ff1_ready = sem("e_ff1_ready")
        e_gelu_made = sem("e_gelu_made")
        e_ff2_ready = sem("e_ff2_ready")
        e_y_made = sem("e_y_made")
        y_stored = sem("y_stored")
        flag_summed = sem("flag_summed")
        flag_made = sem("flag_made")

        WEIGHT_LOADS = 4 + 4 + 3
        CONSTS = 10
        HALF = GROUP // 2
        TURNS = TILES // GROUP
        AHEAD = 6
        SEEK = 2
        FIRST_STEADY = len(EARLY)
        PAIRS = (SPARSE - AHEAD - FIRST_STEADY) // 2
        LAST_STEADY = FIRST_STEADY + 2 * PAIRS
        assert FIRST_STEADY % 2 == 0

        x_tiles = x.rearrange("(t p) d -> p t d", p=P)
        q_tiles = q_dram.rearrange("(t p) d -> p t d", p=P)
        adj_tiles = adj.rearrange("(t p) n -> p t n", p=P)
        out_tiles = out.rearrange("(t p) d -> p t d", p=P)

        def one(tiles, t):
            return tiles[:, bass.ds(t, 1), :].rearrange("p a n -> p (a n)")

        def count_before(s, what):
            if isinstance(s, int):
                return sum(what(kind_of(i)) for i in range(s))
            return sum(what(k) for k in EARLY) + what(NARROW) * (s - FIRST_STEADY)

        def chunks_of(kind):
            return kind.chunks

        def rounds_of(kind):
            return kind.rounds

        def takes_of(kind):
            return kind.rounds - 1

        def there(s, ahead):
            return not isinstance(s, int) or s + ahead < SPARSE

        def is_early(s, n):
            return isinstance(s, int) and s < n

        def steady(engine, step):
            for s in range(FIRST_STEADY):
                step(s, s % 2, s // 2)
            with engine.Fori(0, PAIRS) as i:
                for b in range(2):
                    step(2 * i + FIRST_STEADY + b, b, i + FIRST_STEADY // 2)
            for s in range(LAST_STEADY, SPARSE):
                step(s, s % 2, s // 2)

        block = ctx.enter_context(nc.Block())

        @block.sync
        def _(sp):
            x_groups = x.rearrange("(g t p) d -> g p t d", t=GROUP, p=P)
            kv_groups = kv_dram.rearrange("(g t p) d -> g p t d", t=GROUP, p=P)
            q_groups = q_dram.rearrange("(g t p) d -> g p t d", t=GROUP, p=P)

            def group(of, g):
                return of[bass.ds(g, 1)].rearrange("a p t d -> p (a t) d")

            for b in range(2):
                sp.dma_start(x_grp[b], x_groups[b]).then_inc(x_in[b], 16)
            sp.dma_start(w_qkv_sb[:], w_qkv).then_inc(weights_in, 16)
            for i, v in enumerate((g1, be1, g2, be2)):
                sp.dma_start(norm_cols[:, i:i + 1], v.rearrange("(p a) -> p a", a=1)).then_inc(weights_in, 16)
            sp.dma_start(w_proj_sb[:], w_proj).then_inc(weights_in, 16)
            sp.dma_start(w1_sb[:], w1).then_inc(weights_in, 16)
            sp.dma_start(w2_sb[:], w2.rearrange("(b p) d -> p b d", p=P)).then_inc(weights_in, 16)
            sp.dma_start(bias_rows[:, 0:D], b_proj.rearrange("(a d) -> a d", a=1)).then_inc(weights_in, 16)
            sp.dma_start(bias_rows[:, D:2 * D], b2.rearrange("(a d) -> a d", a=1)).then_inc(weights_in, 16)
            sp.dma_start(bias_rows[:, 2 * D:], b1.rearrange("(a d) -> a d", a=1)).then_inc(weights_in, 16)
            for s in range(2):
                sp.dma_start(adj_sb[s][:], one(adj_tiles, s + 1)).then_inc(adj_in[s], 16)

            def project_pair(i, last=False):
                for b in range(2):
                    g = 2 * i + b
                    if not last:
                        sp.wait_ge(p_norm_made, g + 1)
                        sp.dma_start(x_grp[b], group(x_groups, g + 2)).then_inc(x_in[b], 16)
                    sp.wait_ge(p_kv_kept[0], g + 1)
                    sp.wait_ge(p_kv_kept[1], g + 1)
                    sp.dma_start(group(kv_groups, g), kv_stage[b]).then_inc(kv_stored[b], 16)
                    sp.wait_ge(p_q_kept, g + 1)
                    sp.dma_start(group(q_groups, g), q_stage[b].rearrange("p (t d) -> p t d", t=GROUP)
                                 ).then_inc(q_stored[b], 16)

            with sp.Fori(0, GROUPS // 2 - 1) as i:
                project_pair(i)
            project_pair(GROUPS // 2 - 1, True)

            for b in range(2):
                sp.wait_ge(q_stored[b], 16 * (GROUPS // 2))
                sp.wait_ge(kv_stored[b], 16 * (GROUPS // 2))
            sp.wait_ge(p_values_kept, GROUPS)
            sp.dma_start(adj_landing, one(adj_tiles, 0)).then_inc(d_adj_in, 16)
            sp.dma_start(q_rows_d[:], one(q_tiles, 0)).then_inc(d_q_in, 16)
            for s in range(2):
                sp.dma_start(q_tile[s][:], one(q_tiles, s + 1)).then_inc(q_in[s], 16)

            def load_adjacency(s, b):
                sp.wait_ge(squares_made, 2 * (s - 1))
                sp.dma_start(adj_sb[b][:], one(adj_tiles, s + 1)).then_inc(adj_in[b], 16)

            for s in range(2, AHEAD):
                load_adjacency(s, s % 2)

            def load_x(n, t):
                if not is_early(n, 1):
                    sp.wait_ge(e_x2_made, n)
                sp.dma_start(x_tile[:], one(x_tiles, t)).then_inc(xt_in, 16)

            def store(n, t):
                sp.wait_ge(e_y_made, n + 1)
                sp.dma_start(one(out_tiles, t), y_tile[:]).then_inc(y_stored, 16)

            def step(s, b, r):
                load_x(s, s + 1)
                if there(s, 2):
                    sp.wait_ge(prod_made, s + 1)
                    sp.dma_start(q_tile[b][:], one(q_tiles, s + 3)).then_inc(q_in[b], 16)
                if not is_early(s, 2):
                    store(s - 2, s - 1)
                if there(s, AHEAD):
                    load_adjacency(s + AHEAD, b)

            steady(sp, step)
            load_x(SPARSE, 0)
            store(SPARSE - 2, TILES - 2)
            store(SPARSE - 1, TILES - 1)
            store(SPARSE, 0)
            sp.wait_ge(y_stored, 16 * TILES)
            sp.wait_ge(flag_made, 1)
            with sp.If(sp.value_load(dense_needed[0:1, 0:1], min_val=0, max_val=P) > 0):
                with sp.Fori(0, TILES) as t:
                    sp.wait_ge(d_out_ready, (t + 1) * HEADS)
                    sp.dma_start(adj_landing, one(adj_tiles, t)).then_inc(d_adj_in, 16)
                    sp.wait_ge(d_q_turned, t + 1)
                    sp.dma_start(q_rows_d[:], one(q_tiles, t)).then_inc(d_q_in, 16)
                    load_x(TILES + t, t)
                    store(TILES + t, t)
                sp.wait_ge(y_stored, 16 * 2 * TILES)

        @block.gpsimd
        def _(pool):
            nc.gpsimd.memset(ident[:], 0.0).then_inc(const_step, 1)
            nc.gpsimd.memset(head_mask[:], 1.0).then_inc(const_step, 1)
            nc.gpsimd.memset(fold_weights[:].rearrange("p k q -> p (k q)"), 0.0).then_inc(const_step, 1)
            nc.gpsimd.iota(position_low, [[0, 2], [1, BANK // 2]], base=0, channel_multiplier=0
                           ).then_inc(const_step, 1)
            nc.gpsimd.iota(position_high, [[BANK // 2, 2], [0, BANK // 2]], base=0, channel_multiplier=0
                           ).then_inc(const_step, 1)
            nc.gpsimd.memset(ones_row[:], 1.0).then_inc(consts_made, 1)
            nc.gpsimd.memset(ones_col[:], 1.0).then_inc(consts_made, 1)
            nc.gpsimd.memset(ones_bf[:], 1.0).then_inc(consts_made, 1)
            nc.gpsimd.memset(eps_col[:], EPS).then_inc(consts_made, 1)
            pool.wait_ge(const_step, 5)
            nc.gpsimd.affine_select(out=ident[:], in_=ident[:], compare_op=ALU.not_equal, fill=1.0, base=0,
                                    pattern=[[-1, P]], channel_multiplier=1).then_inc(consts_made, 1)
            for k in range(FOLDS):
                ins = nc.gpsimd.affine_select(out=fold_weights[:, k, :], in_=fold_weights[:, k, :],
                                              compare_op=ALU.not_equal, fill=float(BANK << k), base=0,
                                              pattern=[[-1, P]], channel_multiplier=1)
            ins.then_inc(consts_made, 1)
            nc.gpsimd.tensor_copy(position[:, 0, :], position_low).then_inc(consts_made, 1)
            nc.gpsimd.tensor_copy(position[:, 1, :], position_high).then_inc(consts_made, 1)
            for k in range(FOLDS):
                ins = nc.gpsimd.memset(fold_bit[:, k:k + 1], (BANK << k) + BANK - 1)
            ins.then_inc(consts_made, 1)
            nc.gpsimd.affine_select(out=head_mask[:], in_=head_mask[:], compare_op=ALU.is_ge, fill=0.0, base=0,
                                    pattern=[[-HD, HEADS]], channel_multiplier=1).then_inc(const_step, 1)
            pool.wait_ge(const_step, 6)
            nc.gpsimd.affine_select(out=head_mask[:], in_=head_mask[:], compare_op=ALU.is_ge, fill=0.0, base=HD - 1,
                                    pattern=[[HD, HEADS]], channel_multiplier=-1).then_inc(consts_made, 1)
            for b in range(2):
                nc.gpsimd.memset(gathered[b][:].rearrange("p s d -> p (s d)"), 0.0).then_inc(ring_clear, 1)

            def project_pair(i):
                for b in range(2):
                    g = 2 * i + b
                    pool.wait_ge(p_kv_kept[0], g + 1)
                    pool.wait_ge(p_kv_kept[1], g + 1)
                    pool.sem_inc(pool_past, 1)
                    nc.gpsimd.tensor_copy(values[:, bass.ds(g * GROUP, GROUP), :], kv_stage[b][:, :, D:2 * D]
                                          ).then_inc(p_values_kept, 1)

            with pool.Fori(0, GROUPS // 2) as i:
                project_pair(i)

            for b in range(2):
                pool.wait_ge(kv_stored[b], 16 * (GROUPS // 2))
            pool.wait_ge(ring_clear, 2)

            def gather(s, b, r):
                pool.wait_ge(index_made, s + 1)
                if not is_early(s, 2):
                    pool.wait_ge(sum_ready, s - 1)
                pool.sem_inc(pool_past, 1)
                for j in range(kind_of(s).slots):
                    pool.indirect_dma_start(gathered[b][:, j, :], None, kv_dram,
                                            bass.IndirectOffsetOnAxis(ap=index[b][:, j:j + 1], axis=0),
                                            bounds_check=N - 1, oob_is_err=False).then_inc(kv_in[b], 16)

            steady(pool, gather)

        @block.tensor
        def _(pe):
            pe.wait_ge(consts_made, CONSTS)
            pe.wait_ge(weights_in, 16 * WEIGHT_LOADS)

            def project_pair(i, first=False):
                for b in range(2):
                    g = 2 * i + b
                    pe.wait_ge(p_norm_made, g + 1)
                    for t in range(GROUP):
                        mm = nc.tensor.transpose(ps_s[b][:, t * P:(t + 1) * P], x_nrm[b][:, t, :], ident[:])
                    mm.then_inc(p_norm_turned, 1)
                    pe.wait_ge(p_h_made, g + 1)
                    for half in range(2):
                        if not (first and b == 0):
                            pe.wait_ge(p_kv_kept[half], g)
                        for u in range(HALF):
                            t = half * HALF + u
                            mm = nc.tensor.matmul(ps_t[half][:, u * 2 * D:(u + 1) * 2 * D],
                                                  h_t[b][:, t * P:(t + 1) * P], w_qkv_sb[:, D:3 * D],
                                                  start=True, stop=True)
                        mm.then_inc(p_kv_ready[half], 1)
                    if not (first and b == 0):
                        pe.wait_ge(p_q_kept, g)
                    for t in range(GROUP):
                        mm = nc.tensor.matmul(ps_o[:, t * P:(t + 1) * P], h_t[b][:, t * P:(t + 1) * P],
                                              w_qkv_sb[:, 0:D], start=True, stop=True)
                    mm.then_inc(p_q_ready, 1)
                    if not (first and b == 0):
                        pe.wait_ge(p_keys_kept, g)
                    nc.tensor.matmul(ps_e[:], w_qkv_sb[:, D:2 * D], h_t[b], start=True, stop=True
                                     ).then_inc(p_keys_ready, 1)

            project_pair(0, True)
            with pe.Fori(1, GROUPS // 2) as i:
                project_pair(i)
            for half in range(2):
                pe.wait_ge(p_kv_kept[half], GROUPS)
            pe.wait_ge(p_q_kept, GROUPS)
            pe.wait_ge(p_keys_kept, GROUPS)

            def codes(s):
                pe.wait_ge(nonzero_made, 2 * (s + 1))
                if not is_early(s, 1):
                    pe.wait_ge(cands_found, count_before(s, chunks_of))
                for k in range(FOLDS):
                    nc.tensor.matmul(ps_c[:], fold_weights[:, k, :], nonzero[:, k * BANK:(k + 1) * BANK],
                                     start=(k == 0), stop=False)
                for a in range(2):
                    mm = nc.tensor.matmul(ps_c[:], ones_bf[:], position[:, a, :], start=False, stop=(a == 1))
                mm.then_inc(codes_ready, 1)

            def sum_slots(s, b):
                pe.wait_ge(weighted_made, s + 1)
                if not is_early(s, 1):
                    pe.wait_ge(attn_made, s)
                slots = kind_of(s).slots
                for j in range(slots):
                    mm = nc.tensor.matmul(ps_a[:, 0:D], ident[:], gathered[b][:, j, D:2 * D],
                                          start=(j == 0), stop=(j == slots - 1))
                mm.then_inc(sum_ready, 1)

            def tail_turn(n, rows):
                if not is_early(n, 1):
                    pe.wait_ge(e_y_made, n)
                nc.tensor.transpose(ps_e[:, 0:P], rows[:], ident[:]).then_inc(e_attn_turned, 1)

            def tail_project(n):
                pe.wait_ge(e_attn_t_kept, n + 1)
                nc.tensor.matmul(ps_e[:, 0:D], attn_t[:], w_proj_sb[:], start=True, stop=False)
                nc.tensor.matmul(ps_e[:, 0:D], ones_row[:], bias_rows[:, 0:D], start=False, stop=True
                                 ).then_inc(e_proj_ready, 1)

            def tail_feed(n):
                pe.wait_ge(e_norm_made, n + 1)
                nc.tensor.transpose(ps_e[:, 0:P], x2_norm[:], ident[:]).then_inc(e_norm_turned, 1)
                pe.wait_ge(e_h2_made, n + 1)
                for f in range(FB):
                    nc.tensor.matmul(ps_e[:, f * P:(f + 1) * P], w1_sb[:, f * P:(f + 1) * P], h2_t[:],
                                     start=True, stop=False)
                    mm = nc.tensor.matmul(ps_e[:, f * P:(f + 1) * P],
                                          bias_rows[:, 2 * D + f * P:2 * D + (f + 1) * P], ones_row[:],
                                          start=False, stop=True)
                mm.then_inc(e_ff1_ready, 1)
                pe.wait_ge(e_gelu_made, n + 1)
                for f in range(FB):
                    nc.tensor.matmul(ps_e[:, 0:D], gelu[:, f * P:(f + 1) * P], w2_sb[:, f, :],
                                     start=(f == 0), stop=False)
                nc.tensor.matmul(ps_e[:, 0:D], ones_row[:], bias_rows[:, D:2 * D], start=False, stop=True
                                 ).then_inc(e_ff2_ready, 1)

            def dense_begin(n):
                pe.wait_ge(d_q_in, 16 * (n + 1))
                if not is_early(n, 1):
                    pe.wait_ge(d_attn_made, n * HEADS)
                nc.tensor.transpose(ps_o[:, P:2 * P], q_rows_d[:], ident[:]).then_inc(d_q_turned, 1)

            def dense_head(k, h, first=False):
                pe.wait_ge(d_q_head, k + 1)
                for c in range(CHUNKS):
                    if not (first and c < 2):
                        pe.wait_ge(d_scores_masked, k * CHUNKS + c - 1)
                    nc.tensor.matmul(ps_s[c % 2][:], q_head[:], keys_t[:, c * BANK:(c + 1) * BANK],
                                     start=True, stop=True).then_inc(d_scores_ready, 1)
                pe.wait_ge(d_probs_made, k + 1)
                for j in range(TURNS):
                    if not (first and j < 2):
                        pe.wait_ge(d_turned_kept[j % 2], k * (TURNS // 2) + j // 2)
                    for u in range(GROUP):
                        c = j * GROUP + u
                        mm = nc.tensor.transpose(ps_t[j % 2][:, u * P:(u + 1) * P], scores[:, c * P:(c + 1) * P], ident[:])
                    mm.then_inc(d_probs_turned, 1)
                for j in range(2):
                    pe.wait_ge(d_turned_kept[j], (k + 1) * (TURNS // 2))
                if not first:
                    pe.wait_ge(d_attn_made, k)
                for c in range(TILES):
                    mm = nc.tensor.matmul(ps_o[:, 0:HD], probs_t[:, c, :], values[:, c, bass.ds(h * HD, HD)],
                                          start=(c == 0), stop=(c == TILES - 1))
                mm.then_inc(d_out_ready, 1)

            for s in range(3):
                codes(s)
            pe.wait_ge(p_values_kept, GROUPS)
            dense_begin(0)
            dense_head(0, 0, True)
            with pe.Fori(1, HEADS) as h:
                dense_head(h, h)

            def step(s, b, r):
                if not is_early(s, 1):
                    pe.wait_ge(attn_made, s)
                    tail_turn(s - 1, attn)
                if there(s, 3):
                    codes(s + 3)
                if not is_early(s, 1):
                    tail_project(s - 1)
                    tail_feed(s - 1)
                sum_slots(s, b)

            steady(pe, step)
            pe.wait_ge(attn_made, SPARSE)
            tail_turn(SPARSE - 1, attn)
            tail_project(SPARSE - 1)
            tail_feed(SPARSE - 1)
            pe.wait_ge(d_attn_made, HEADS)
            tail_turn(SPARSE, attn_d)
            tail_project(SPARSE)
            tail_feed(SPARSE)

            pe.wait_ge(flag_summed, 1)
            pe.wait_ge(e_y_made, TILES)
            nc.tensor.matmul(ps_e[0:1, 0:1], too_many[:], ones_col[:], start=True, stop=True).then_inc(flag_summed, 1)
            pe.wait_ge(flag_made, 1)
            with pe.If(pe.value_load(dense_needed[0:1, 0:1], min_val=0, max_val=P) > 0):
                with pe.Fori(0, TILES) as t:
                    dense_begin(t + 1)
                    with pe.Fori(0, HEADS) as h:
                        dense_head((t + 1) * HEADS + h, h)
                    pe.wait_ge(d_attn_made, (t + 2) * HEADS)
                    tail_turn(TILES + t, attn_d)
                    tail_project(TILES + t)
                    tail_feed(TILES + t)

        @block.scalar
        def _(act):
            act.wait_ge(consts_made, CONSTS)
            act.wait_ge(weights_in, 16 * WEIGHT_LOADS)

            def deviation(g, b):
                act.wait_ge(p_stats_made, g + 1)
                nc.scalar.activation(std[b][:], mean_var[b][:, :, 1], ACT.Sqrt, bias=eps_col[:]).then_inc(p_std_made, 1)

            def project_pair(i, last=False):
                for b in range(2):
                    g = 2 * i + b
                    act.wait_ge(p_norm_turned, g + 1)
                    nc.scalar.activation(h_t[b], ps_s[b][:], ACT.Identity, bias=norm_cols[:, 1:2],
                                         scale=norm_cols[:, 0:1]).then_inc(p_h_made, 1)
                    act.wait_ge(p_kv_ready[1], g + 1)
                    if not (isinstance(i, int) and i == 0):
                        act.wait_ge(kv_stored[b], 16 * i)
                        act.wait_ge(p_values_kept, g - 1)
                    nc.scalar.copy(kv_stage[b][:, HALF:, :].rearrange("p t d -> p (t d)"), ps_t[1][:]
                                   ).then_inc(p_kv_kept[1], 1)
                    act.wait_ge(p_keys_ready, g + 1)
                    nc.scalar.copy(keys_t[:, bass.ds(g * BANK, BANK)], ps_e[:]).then_inc(p_keys_kept, 1)
                    if not last:
                        deviation(g + 2, b)

            deviation(0, 0)
            deviation(1, 1)
            project_pair(0)
            with act.Fori(1, GROUPS // 2 - 1) as i:
                project_pair(i)
            project_pair(GROUPS // 2 - 1, True)

            def square(s, b, r, half):
                if half == 0:
                    act.wait_ge(adj_in[b], 16 * (r + 1))
                    if not is_early(s, 1):
                        act.wait_ge(codes_ready, s)
                cols = slice(half * (N // 2), (half + 1) * (N // 2))
                nc.scalar.activation(nonzero[:, cols], adj_sb[b][:, cols], ACT.Square).then_inc(squares_made, 1)

            def sign(s, half):
                act.wait_ge(squares_made, 2 * s + half + 1)
                cols = slice(half * (N // 2), (half + 1) * (N // 2))
                nc.scalar.activation(nonzero[:, cols], nonzero[:, cols], ACT.Sign).then_inc(nonzero_made, 1)

            def tail_turned(n):
                act.wait_ge(e_attn_turned, n + 1)
                nc.scalar.copy(attn_t[:], ps_e[:, 0:P]).then_inc(e_attn_t_kept, 1)

            def tail_std(n):
                act.wait_ge(e_stats_made, n + 1)
                nc.scalar.activation(e_std[:], e_mean_var[:, 1:2], ACT.Sqrt, bias=eps_col[:]).then_inc(e_std_made, 1)

            def tail_h2(n):
                act.wait_ge(e_norm_turned, n + 1)
                nc.scalar.activation(h2_t[:], ps_e[:, 0:P], ACT.Identity, bias=norm_cols[:, 3:4],
                                     scale=norm_cols[:, 2:3]).then_inc(e_h2_made, 1)

            def tail_gelu(n):
                act.wait_ge(e_ff1_ready, n + 1)
                nc.scalar.activation(gelu[:], ps_e[:], ACT.Gelu_apprx_tanh).then_inc(e_gelu_made, 1)

            def dense_begin(n):
                act.wait_ge(d_q_turned, n + 1)
                nc.scalar.copy(q_t[:], ps_o[:, P:2 * P]).then_inc(d_q_kept, 1)

            def dense_head(k):
                act.wait_ge(d_neg_max, k + 1)
                nc.scalar.activation(scores[:], scores[:], ACT.Exp, bias=neg_max[:], scale=SCALE,
                                     accum_out=row_sum[:]).then_inc(d_probs_made, 1)
                for j in range(0, TURNS, 2):
                    act.wait_ge(d_probs_turned, k * TURNS + j + 1)
                    nc.scalar.copy(probs_t[:, j * GROUP:(j + 1) * GROUP, :].rearrange("p a b -> p (a b)"), ps_t[0][:]
                                   ).then_inc(d_turned_kept[0], 1)

            for s in range(4):
                for half in range(2):
                    square(s, s % 2, s // 2, half)
                for half in range(2):
                    sign(s, half)
            for b in range(2):
                act.wait_ge(kv_stored[b], 16 * (GROUPS // 2))
            act.wait_ge(p_values_kept, GROUPS)
            dense_begin(0)
            dense_head(0)
            with act.Fori(1, HEADS) as h:
                dense_head(h)

            def step(s, b, r):
                if not is_early(s, 1):
                    tail_turned(s - 1)
                if there(s, 4):
                    square(s + 4, b, r + 2, 0)
                if not is_early(s, 1):
                    tail_std(s - 1)
                if there(s, 4):
                    square(s + 4, b, r + 2, 1)
                act.wait_ge(s_sub_made, s + 1)
                slots = kind_of(s).slots
                nc.scalar.activation(p_slot[:, 0:slots, :], s_sub[:, 0:slots, :], ACT.Exp, scale=SCALE
                                     ).then_inc(p_made, 1)
                if there(s, 4):
                    sign(s + 4, 0)
                if not is_early(s, 1):
                    tail_h2(s - 1)
                if there(s, 4):
                    sign(s + 4, 1)
                if not is_early(s, 1):
                    tail_gelu(s - 1)

            steady(act, step)
            for n in (SPARSE - 1, SPARSE):
                tail_turned(n)
                tail_std(n)
                tail_h2(n)
                tail_gelu(n)
            act.wait_ge(flag_made, 1)
            with act.If(act.value_load(dense_needed[0:1, 0:1], min_val=0, max_val=P) > 0):
                with act.Fori(0, TILES) as t:
                    dense_begin(t + 1)
                    with act.Fori(0, HEADS) as h:
                        dense_head((t + 1) * HEADS + h)
                    tail_turned(TILES + t)
                    tail_std(TILES + t)
                    tail_h2(TILES + t)
                    tail_gelu(TILES + t)

        @block.vector
        def _(dve):
            nc.vector.memset(worst_cand[:], 0.0).then_inc(worst_step, 1)
            nc.vector.memset(worst_found[:], 0.0).then_inc(worst_step, 1)

            def statistics(g, b, r):
                dve.wait_ge(x_in[b], 16 * (r + 1))
                for t in range(GROUP):
                    ins = nc.vector.bn_stats(stat6[b][:, t, :], x_grp[b][:, t, :])
                ins.then_inc(p_stat6_made, 1)
                dve.wait_ge(p_stat6_made, g + 1)
                dve.sem_inc(dve_past, 1)
                for t in range(GROUP):
                    ins = nc.vector.bn_aggr(mean_var[b][:, t, :], stat6[b][:, t, :])
                ins.then_inc(p_stats_made, 1)

            def keep(g, b, r, first):
                dve.wait_ge(p_kv_ready[0], g + 1)
                if not first:
                    dve.wait_ge(kv_stored[b], 16 * r)
                    dve.wait_ge(p_values_kept, g - 1)
                nc.vector.tensor_copy(kv_stage[b][:, 0:HALF, :].rearrange("p t d -> p (t d)"), ps_t[0][:]
                                      ).then_inc(p_kv_kept[0], 1)
                dve.wait_ge(p_q_ready, g + 1)
                if not first:
                    dve.wait_ge(q_stored[b], 16 * r)
                nc.vector.tensor_copy(q_stage[b], ps_o[:]).then_inc(p_q_kept, 1)

            def project_pair(i, last=False):
                first = isinstance(i, int) and i == 0
                for b in range(2):
                    g = 2 * i + b
                    dve.wait_ge(p_std_made, g + 1)
                    nc.vector.reciprocal(rstd[b][:], std[b][:]).then_inc(p_rstd_made, 1)
                    dve.wait_ge(p_rstd_made, g + 1)
                    if not first:
                        dve.wait_ge(p_norm_turned, g - 1)
                    for t in range(GROUP):
                        ins = nc.vector.tensor_scalar(x_nrm[b][:, t, :], x_grp[b][:, t, :], mean_var[b][:, t, 0:1],
                                                      rstd[b][:, t:t + 1], ALU.subtract, ALU.mult)
                    ins.then_inc(p_norm_made, 1)
                    if b == 1:
                        keep(g - 1, 0, i, first)
                    elif not first:
                        keep(g - 1, 1, i - 1, isinstance(i, int) and i == 1)
                    if not last:
                        statistics(g + 2, b, i + 1)

            statistics(0, 0, 0)
            statistics(1, 1, 0)
            dve.wait_ge(consts_made, CONSTS)
            project_pair(0)
            project_pair(1)
            with dve.Fori(2, GROUPS // 2 - 1) as i:
                project_pair(i)
            project_pair(GROUPS // 2 - 1, True)
            keep(GROUPS - 1, 1, GROUPS // 2 - 1, False)

            def candidates(s):
                kind = kind_of(s)
                dve.wait_ge(codes_ready, s + 1)
                dve.sem_inc(dve_past, 1)
                for c in range(kind.chunks):
                    nc.vector.max(cand[:, 8 * c:8 * c + 8], ps_c[:, c::kind.chunks]).then_inc(cands_found, 1)

            def candidates_int(s):
                kind = kind_of(s)
                dve.wait_ge(cands_found, count_before(s, chunks_of) + kind.chunks)
                nc.vector.tensor_copy(cand_int[:, 0:kind.cands], cand[:, 0:kind.cands]).then_inc(cands_int, 1)

            def spread_folds(s):
                kind = kind_of(s)
                dve.wait_ge(cands_int, s + 1)
                nc.vector.tensor_tensor(spread[:, 0:kind.cands, :],
                                        cand_int[:, 0:kind.cands].unsqueeze(2).broadcast_to([P, kind.cands, FOLDS]),
                                        fold_bit[:].unsqueeze(1).broadcast_to([P, kind.cands, FOLDS]), ALU.bitwise_and).then_inc(spread_made, 1)

            def note_candidates(s):
                kind = kind_of(s)
                dve.wait_ge(worst_step, 2 * (s + 1))
                nc.vector.tensor_tensor(worst_cand[:, 0:kind.chunks], worst_cand[:, 0:kind.chunks],
                                        cand[:, 7:kind.cands:8], ALU.max).then_inc(worst_step, 1)

            def sources(kind):
                flat = spread[:, 0:kind.cands, :].rearrange("p a b -> p (a b)")
                rest = [r[:, 0:kind.cands * FOLDS] for r in spread_rest]
                return [flat, rest[0], rest[1]]

            def find_round(s, r):
                kind = kind_of(s)
                if r == 0:
                    dve.wait_ge(spread_made, s + 1)
                else:
                    dve.wait_ge(round_taken, count_before(s, takes_of) + r)
                dve.sem_inc(dve_past, 1)
                nc.vector.max(found[:, 8 * r:8 * r + 8], sources(kind)[r]).then_inc(round_found, 1)

            def take_round(s, r):
                kind = kind_of(s)
                dve.wait_ge(round_found, count_before(s, rounds_of) + r + 1)
                dve.sem_inc(dve_past, 1)
                nc.vector.match_replace(sources(kind)[r + 1], found[:, 8 * r:8 * r + 8], sources(kind)[r], 0.0
                                        ).then_inc(round_taken, 1)

            def decode_bias(s, b):
                kind = kind_of(s)
                dve.wait_ge(round_found, count_before(s, rounds_of) + kind.rounds)
                nc.vector.tensor_scalar(slot_bias[b][:, 0:kind.slots], found[:, 0:kind.slots], float(BANK), MASKED,
                                        ALU.is_lt, ALU.mult).then_inc(found_read, 1)
                nc.vector.tensor_copy(found_int[:, 0:kind.slots], found[:, 0:kind.slots]).then_inc(found_read, 1)
                nc.vector.tensor_scalar(fold[:, 0:kind.slots], found[:, 0:kind.slots].bitcast(I32), 23, FOLDS - 1,
                                        ALU.logical_shift_right, ALU.bitwise_and).then_inc(found_read, 1)

            def decode_low(s):
                kind = kind_of(s)
                dve.wait_ge(found_read, 4 * s + 3)
                nc.vector.tensor_scalar(low[:, 0:kind.slots], found_int[:, 0:kind.slots], BANK - 1, None,
                                        ALU.bitwise_and).then_inc(found_read, 1)

            def decode_column(s):
                kind = kind_of(s)
                dve.wait_ge(found_read, 4 * (s + 1))
                nc.vector.scalar_tensor_tensor(column[:, 0:kind.slots], fold[:, 0:kind.slots], float(BANK),
                                               low[:, 0:kind.slots], ALU.mult, ALU.add).then_inc(column_made, 1)

            def decode_index(s, b):
                kind = kind_of(s)
                dve.wait_ge(column_made, s + 1)
                nc.vector.scalar_tensor_tensor(index[b][:, 0:kind.slots], slot_bias[b][:, 0:kind.slots], FAR / MASKED,
                                               column[:, 0:kind.slots], ALU.mult, ALU.add).then_inc(index_made, 1)

            def note_found(s):
                kind = kind_of(s)
                dve.wait_ge(worst_step, 2 * (s + 1) + 1)
                nc.vector.tensor_tensor(worst_found[:], worst_found[:], found[:, kind.slots - 1:kind.slots],
                                        ALU.max).then_inc(worst_step, 1)

            def products(s, b, r):
                slots = kind_of(s).slots
                dve.wait_ge(kv_in[b], 16 * gathers_until(s, b, r))
                dve.wait_ge(q_in[b], 16 * (r + 1))
                nc.vector.tensor_tensor(prod[:, 0:slots, :], gathered[b][:, 0:slots, 0:D],
                                        q_tile[b][:].unsqueeze(1).broadcast_to([P, slots, D]), ALU.mult
                                        ).then_inc(prod_made, 1)

            def scores_of_slots(s):
                slots = kind_of(s).slots
                dve.wait_ge(prod_made, s + 1)
                nc.vector.tensor_reduce(s_raw[:, 0:slots, :].rearrange("p s h -> p (s h)"),
                                        prod[:, 0:slots, :].rearrange("p s (h d) -> p (s h) d", d=HD), AX.X, ALU.add
                                        ).then_inc(s_raw_made, 1)

            def mask_slots(s, b):
                slots = kind_of(s).slots
                dve.wait_ge(s_raw_made, s + 1)
                nc.vector.tensor_tensor(s_msk[:, 0:slots, :], s_raw[:, 0:slots, :],
                                        slot_bias[b][:, 0:slots].unsqueeze(2).broadcast_to([P, slots, HEADS]), ALU.add
                                        ).then_inc(s_msk_made, 1)

            def max_slots(s):
                slots = kind_of(s).slots
                dve.wait_ge(s_msk_made, s + 1)
                nc.vector.tensor_reduce(s_max[:], s_msk[:, 0:slots, :].rearrange("p s h -> p h s"), AX.X, ALU.max
                                        ).then_inc(s_max_made, 1)

            def subtract_max(s):
                slots = kind_of(s).slots
                dve.wait_ge(s_max_made, s + 1)
                nc.vector.tensor_tensor(s_sub[:, 0:slots, :], s_msk[:, 0:slots, :],
                                        s_max[:].unsqueeze(1).broadcast_to([P, slots, HEADS]), ALU.subtract
                                        ).then_inc(s_sub_made, 1)

            def weigh_values(s, b):
                slots = kind_of(s).slots
                dve.wait_ge(p_made, s + 1)
                nc.vector.tensor_reduce(p_sum[:], p_slot[:, 0:slots, :].rearrange("p s h -> p h s"), AX.X, ALU.add
                                        ).then_inc(p_sum_made, 1)
                v = gathered[b][:, 0:slots, D:2 * D].rearrange("p s (h d) -> p s h d", d=HD)
                nc.vector.tensor_tensor(v, v, p_slot[:, 0:slots, :].unsqueeze(3).broadcast_to([P, slots, HEADS, HD]),
                                        ALU.mult).then_inc(weighted_made, 1)
                dve.wait_ge(p_sum_made, s + 1)
                nc.vector.reciprocal(inv_sum[:], p_sum[:]).then_inc(inv_sum_made, 1)

            def finish_attention(s):
                dve.wait_ge(inv_sum_made, s + 1)
                dve.wait_ge(sum_ready, s + 1)
                if not is_early(s, 1):
                    dve.wait_ge(e_attn_turned, s)
                nc.vector.tensor_tensor(attn[:].rearrange("p (h d) -> p h d", d=HD),
                                        ps_a[:, 0:D].rearrange("p (h d) -> p h d", d=HD),
                                        inv_sum[:].unsqueeze(2).broadcast_to([P, HEADS, HD]), ALU.mult
                                        ).then_inc(attn_made, 1)

            def tail_residual(n):
                dve.wait_ge(xt_in, 16 * (n + 1))
                dve.wait_ge(e_proj_ready, n + 1)
                nc.vector.tensor_tensor(x2[:], ps_e[:, 0:D], x_tile[:], ALU.add).then_inc(e_x2_made, 1)

            def tail_stat6(n):
                dve.wait_ge(e_x2_made, n + 1)
                nc.vector.bn_stats(e_stat6[:], x2[:]).then_inc(e_stat6_made, 1)

            def tail_stats(n):
                dve.wait_ge(e_stat6_made, n + 1)
                dve.sem_inc(dve_past, 1)
                nc.vector.bn_aggr(e_mean_var[:], e_stat6[:]).then_inc(e_stats_made, 1)

            def tail_rstd(n):
                dve.wait_ge(e_std_made, n + 1)
                nc.vector.reciprocal(e_rstd[:], e_std[:]).then_inc(e_rstd_made, 1)

            def tail_norm(n):
                dve.wait_ge(e_rstd_made, n + 1)
                nc.vector.tensor_scalar(x2_norm[:], x2[:], e_mean_var[:, 0:1], e_rstd[:], ALU.subtract, ALU.mult
                                        ).then_inc(e_norm_made, 1)

            def tail_end(n):
                dve.wait_ge(e_ff2_ready, n + 1)
                if not is_early(n, 1):
                    dve.wait_ge(y_stored, 16 * n)
                nc.vector.tensor_tensor(y_tile[:], ps_e[:, 0:D], x2[:], ALU.add).then_inc(e_y_made, 1)

            def dense_begin(n):
                dve.wait_ge(d_adj_in, 16 * (n + 1))
                nc.vector.tensor_scalar(mask_bias[:], adj_landing, 0.0, MASKED, ALU.is_equal, ALU.mult
                                        ).then_inc(d_bias_made, 1)
                dve.wait_ge(d_bias_made, n + 1)
                dve.wait_ge(d_q_kept, n + 1)
                dve.sem_inc(dve_past, 1)

            def dense_head(k, h, first=False):
                if not first:
                    dve.wait_ge(d_scores_ready, k * CHUNKS)
                nc.vector.tensor_scalar(q_head[:], q_t[:], head_mask[:, bass.ds(h, 1)], None, ALU.mult
                                        ).then_inc(d_q_head, 1)
                if not first:
                    dve.wait_ge(d_probs_turned, k * TURNS)
                    dve.sem_inc(dve_past, 1)
                for c in range(CHUNKS):
                    dve.wait_ge(d_scores_ready, k * CHUNKS + c + 1)
                    dve.sem_inc(dve_past, 1)
                    nc.vector.tensor_tensor_reduce(
                        scores[:, c * BANK:(c + 1) * BANK], ps_s[c % 2][:], mask_bias[:, c * BANK:(c + 1) * BANK],
                        1.0, MASKED, ALU.add, ALU.max, chunk_max[:, c:c + 1]).then_inc(d_scores_masked, 1)
                dve.wait_ge(d_scores_masked, (k + 1) * CHUNKS)
                nc.vector.tensor_reduce(row_max[:], chunk_max[:], AX.X, ALU.max).then_inc(d_row_max, 1)
                dve.wait_ge(d_row_max, k + 1)
                nc.vector.tensor_scalar(neg_max[:], row_max[:], -SCALE, None, ALU.mult).then_inc(d_neg_max, 1)
                for j in range(1, TURNS, 2):
                    dve.wait_ge(d_probs_turned, k * TURNS + j + 1)
                    nc.vector.tensor_copy(probs_t[:, j * GROUP:(j + 1) * GROUP, :].rearrange("p a b -> p (a b)"),
                                          ps_t[1][:]).then_inc(d_turned_kept[1], 1)
                dve.wait_ge(d_probs_made, k + 1)
                nc.vector.reciprocal(inv_sum_d[:], row_sum[:]).then_inc(d_inv_sum, 1)
                dve.wait_ge(d_inv_sum, k + 1)
                dve.wait_ge(d_out_ready, k + 1)
                nc.vector.tensor_scalar(attn_d[:, bass.ds(h * HD, HD)], ps_o[:, 0:HD], inv_sum_d[:], None, ALU.mult
                                        ).then_inc(d_attn_made, 1)

            def search(s, b):
                candidates(s)
                candidates_int(s)
                spread_folds(s)
                note_candidates(s)
                rounds = kind_of(s).rounds
                for r in range(rounds):
                    find_round(s, r)
                    if r + 1 < rounds:
                        take_round(s, r)
                decode_bias(s, b)
                decode_low(s)
                decode_column(s)
                decode_index(s, b)
                note_found(s)

            search(0, 0)
            search(1, 1)
            for b in range(2):
                dve.wait_ge(q_stored[b], 16 * (GROUPS // 2))
            dense_begin(0)
            dense_head(0, 0, True)
            with dve.Fori(1, HEADS) as h:
                dense_head(h, h)

            def step(s, b, r):
                ahead = there(s, SEEK)
                c = s + SEEK
                rounds = kind_of(c).rounds if ahead else 0
                tail = not is_early(s, 1)
                if ahead:
                    candidates(c)
                if tail:
                    finish_attention(s - 1)
                if ahead:
                    candidates_int(c)
                products(s, b, r)
                if ahead:
                    spread_folds(c)
                if tail:
                    tail_residual(s - 1)
                scores_of_slots(s)
                if ahead:
                    note_candidates(c)
                if tail:
                    tail_stat6(s - 1)
                if ahead:
                    find_round(c, 0)
                if tail:
                    tail_stats(s - 1)
                mask_slots(s, b)
                if ahead:
                    take_round(c, 0)
                max_slots(s)
                if ahead:
                    find_round(c, 1)
                subtract_max(s)
                if rounds == 3:
                    take_round(c, 1)
                    find_round(c, 2)
                if tail:
                    tail_rstd(s - 1)
                if ahead:
                    decode_bias(c, b)
                if tail:
                    tail_norm(s - 1)
                if ahead:
                    decode_low(c)
                    decode_column(c)
                    note_found(c)
                    decode_index(c, b)
                weigh_values(s, b)
                if tail:
                    tail_end(s - 1)

            steady(dve, step)
            finish_attention(SPARSE - 1)
            for n in (SPARSE - 1, SPARSE):
                tail_residual(n)
                tail_stat6(n)
                tail_stats(n)
                tail_rstd(n)
                tail_norm(n)
                tail_end(n)

            dve.wait_ge(worst_step, 2 * (SPARSE + 1))
            nc.vector.tensor_reduce(worst[:, 0:1], worst_cand[:], AX.X, ALU.max).then_inc(worst_step, 1)
            nc.vector.tensor_copy(worst[:, 1:2], worst_found[:]).then_inc(worst_step, 1)
            dve.wait_ge(worst_step, 2 * (SPARSE + 2))
            nc.vector.tensor_scalar(worst[:], worst[:], float(BANK), None, ALU.is_ge).then_inc(worst_step, 1)
            dve.wait_ge(worst_step, 2 * (SPARSE + 2) + 1)
            nc.vector.tensor_reduce(too_many[:], worst[:], AX.X, ALU.max).then_inc(flag_summed, 1)
            dve.wait_ge(flag_summed, 2)
            nc.vector.tensor_copy(dense_needed[:], ps_e[0:1, 0:1]).then_inc(flag_made, 1)
            dve.wait_ge(flag_made, 1)
            with dve.If(dve.value_load(dense_needed[0:1, 0:1], min_val=0, max_val=P) > 0):
                with dve.Fori(0, TILES) as t:
                    dense_begin(t + 1)
                    with dve.Fori(0, HEADS) as h:
                        dense_head((t + 1) * HEADS + h, h)
                    tail_residual(TILES + t)
                    tail_stat6(TILES + t)
                    tail_stats(TILES + t)
                    tail_rstd(TILES + t)
                    tail_norm(TILES + t)
                    tail_end(TILES + t)


NAMES = ["x", "adj"] + [f"L0_gnn_{n}" for n in
                        ("w_qkv", "w_proj", "b_proj", "w1", "b1", "w2", "b2", "g1", "be1", "g2", "be2")]


def kernel(**inputs):
    import numpy as np
    import concourse.bacc as bacc
    from concourse.bass_utils import run_bass_kernel_spmd

    nc = bacc.Bacc("TRN2", target_bir_lowering=False, num_devices=1)
    arrays, args = {}, []
    for name in NAMES:
        a = np.ascontiguousarray(inputs[name])
        arrays[f"in_{name}"] = a
        args.append(nc.dram_tensor(f"in_{name}", a.shape, mybir.dt.from_np(a.dtype), kind="ExternalInput").ap())
    out = nc.dram_tensor("out_0", inputs["x"].shape, F32, kind="ExternalOutput").ap()
    graph_layer(nc, *args, out)
    result = run_bass_kernel_spmd(nc, [arrays], core_ids=[0])
    return result.results[0]["out_0"]
```

```python
from contextlib import ExitStack

import concourse.bass as bass
from concourse import mybir

ALU = mybir.AluOpType
ACT = mybir.ActivationFunctionType
AX = mybir.AxisListType
F32 = mybir.dt.float32
BF16 = mybir.dt.bfloat16
I32 = mybir.dt.int32
U32 = mybir.dt.uint32

P = 128
BANK = 512
HEADS = 8
EPS = 1e-5
MASKED = -1e30
FAR = 1 << 20
HEAVY = P // HEADS
PARTS_OF_TILE = P // HEAVY


class Kind:

    def __init__(self, chunks, slots):
        self.chunks, self.slots = chunks, slots
        self.rounds = slots // 8 + 1
        self.cands = 8 * chunks


def graph_layer(nc, x, adj, w_qkv, w_proj, b_proj, w1, b1, w2, b2, g1, be1, g2, be2, out):
    N, D = x.shape
    FF = w1.shape[1]
    HD = D // HEADS
    SCALE = float(HD) ** -0.5
    TILES = N // P
    GROUP = BANK // P
    GROUPS = TILES // GROUP
    CHUNKS = N // BANK
    FB = FF // P
    FOLDS = N // BANK
    assert D == P and FOLDS == 8 and FF == BANK

    NARROW = Kind(4, 11)
    EARLY = [Kind(8, 23), Kind(8, 21), Kind(16, 31)] + 4 * [Kind(4, 13)] + [NARROW]
    LATE = [Kind(4, 10)] + 2 * [Kind(4, 9)] + 3 * [Kind(4, 8)]
    MAX_SLOTS = max(k.slots for k in EARLY)
    MAX_FOUND = 8 * max(k.rounds for k in EARLY)
    EARLY_AT = [8, 36, 0, 31, 44, 0, 13, 31]
    PLACES = [44, 0, 13, 31]
    DEPTH = len(PLACES)
    MAX_CANDS = max(k.cands for k in EARLY)
    RING_SLOTS = max(at + k.slots for at, k in zip(EARLY_AT, EARLY))

    FIRST_TILES = [1, 2, 0]
    HEAVY_STEP = FIRST_TILES.index(0)

    def tile_of(s):
        return FIRST_TILES[s] if isinstance(s, int) and s < len(FIRST_TILES) else s

    def is_heavy(s):
        return isinstance(s, int) and s == HEAVY_STEP

    def kind_of(s):
        if isinstance(s, int) and s < len(EARLY):
            return EARLY[s]
        if isinstance(s, int) and s >= TILES - len(LATE):
            return LATE[s - (TILES - len(LATE))]
        return NARROW

    def slots_in_ring(s, q):
        at = EARLY_AT[s] if isinstance(s, int) and s < len(EARLY) else PLACES[q]
        return slice(at, at + kind_of(s).slots)

    def last_in_slot(s, j):
        at = slots_in_ring(s, s % DEPTH).start + j
        there = [t + 1 for t in range(s) if at in range(*slots_in_ring(t, t % DEPTH).indices(RING_SLOTS))]
        return max(there, default=0)

    def weighed_before(s):
        if not isinstance(s, int):
            return s - (DEPTH - 1)
        return max(last_in_slot(s, j) for j in range(kind_of(s).slots))

    assert all(weighed_before(s) <= s - (DEPTH - 1) for s in range(len(EARLY), TILES))

    def gathers_until(s, i, q):
        if isinstance(s, int):
            return sum(kind_of(t).slots for t in range(q, s + 1, DEPTH))
        return NARROW.slots * i + (NARROW.slots + sum(k.slots for k in EARLY[q::DEPTH]))

    kv_dram = nc.dram_tensor("keys_values", (N, 2 * D), F32).ap()
    q_dram = nc.dram_tensor("queries", (N, D), F32).ap()

    with ExitStack() as ctx:
        def sb(name, shape, dt=F32):
            return ctx.enter_context(nc.sbuf_tensor(name, shape, dt))

        def psum(name):
            return ctx.enter_context(nc.psum_tensor(name, [P, BANK], F32))

        def sem(name):
            return ctx.enter_context(nc.semaphore(name))

        w_qkv_sb = sb("w_qkv_sb", [P, 3 * D])
        w_proj_sb = sb("w_proj_sb", [P, D])
        w1_sb = sb("w1_sb", [P, FF])
        w2_sb = sb("w2_sb", [P, FB, D])
        norm_cols = sb("norm_cols", [P, 4])
        bias_rows = sb("bias_rows", [1, 2 * D])
        b1_blocks = sb("b1_blocks", [FB, P])
        block_cols = sb("block_cols", [FB, FB, P])
        ones_row = sb("ones_row", [1, P])
        ones_col = sb("ones_col", [P, 1])
        zero_col = sb("zero_col", [P, 1])
        eps_col = sb("eps_col", [P, 1])
        ident = sb("ident", [P, P])
        head_mask = sb("head_mask", [P, HEADS])
        fold_weights = sb("fold_weights", [P, FOLDS, P], BF16)
        position = sb("position", [1, 2, BANK], BF16)
        ones_bf = sb("ones_bf", [1, P], BF16)
        fold_bit = sb("fold_bit", [P, FOLDS], I32)
        pack_mask = sb("pack_mask", [P, HEADS])
        PLACE = P - HEAVY
        place = sb("place", [P, PLACE + P])
        light_rows = sb("light_rows", [P, 1])

        keys_t = sb("keys_t", [P, N])
        values = sb("values", [P, TILES, D])

        mask_bias = sb("mask_bias", [P, N], BF16)
        scores = sb("scores", [P, N])
        probs_t = sb("probs_t", [P, TILES, P])
        q_rows_d = sb("q_rows_d", [P, D])
        q_t = sb("q_t", [P, P])
        q_pack = sb("q_pack", [P, HEADS, HEAVY])
        chunk_max = sb("chunk_max", [P, CHUNKS])
        row_max = sb("row_max", [P, 1])
        neg_max = sb("neg_max", [P, 1])
        row_sum = sb("row_sum", [P, 1])
        inv_sum_d = sb("inv_sum_d", [P, 1])
        attn_d = sb("attn_d", [P, D])

        def group_buf(whole, at, width):
            return whole[:, at * BANK:(at + width) * BANK]

        probs_flat = probs_t[:].rearrange("p a b -> p (a b)")
        x_grp = [group_buf(scores, b, 1).rearrange("p (t d) -> p t d", t=GROUP) for b in range(2)]
        x_nrm = [group_buf(scores, 2 + b, 1).rearrange("p (t d) -> p t d", t=GROUP) for b in range(2)]
        h_t = [group_buf(scores, 4 + b, 1) for b in range(2)]
        q_stage = [group_buf(scores, 6 + b, 1) for b in range(2)]
        kv_stage = [group_buf(probs_flat, 2 * b, 2).rearrange("p (t d) -> p t d", t=GROUP) for b in range(2)]
        stat6 = [sb(f"stat6_{b}", [P, GROUP, 6]) for b in range(2)]
        mean_var = [sb(f"mean_var{b}", [P, GROUP, 2]) for b in range(2)]
        std = [sb(f"std{b}", [P, GROUP]) for b in range(2)]
        rstd = [sb(f"rstd{b}", [P, GROUP]) for b in range(2)]

        adj_sb = [sb(f"adj_sb{b}", [P, N], I32) for b in range(2)]
        nonzero = sb("nonzero", [P, N], BF16)
        cand = sb("cand", [P, MAX_CANDS])
        cand_int = sb("cand_int", [P, MAX_CANDS], I32)
        spread = sb("spread", [P, MAX_CANDS, FOLDS], I32)
        spread_rest = sb("spread_rest", [P, MAX_CANDS * FOLDS], I32)
        position_low, position_high = spread_rest[0:1, 0:BANK], spread_rest[0:1, BANK:2 * BANK]
        packed = spread_rest[:, 0:D].bitcast(F32).rearrange("p (h d) -> p h d", d=HD)
        found = sb("found", [P, MAX_FOUND])
        found_int = sb("found_int", [P, MAX_SLOTS], I32)
        low = sb("low", [P, MAX_SLOTS], I32)
        fold = sb("fold", [P, MAX_SLOTS], I32)
        column = sb("column", [P, MAX_SLOTS])
        slot_bias = [sb(f"slot_bias{q}", [P, MAX_SLOTS]) for q in range(DEPTH)]
        index = [sb(f"index{q}", [P, MAX_SLOTS], U32) for q in range(DEPTH)]
        worst_cand = sb("worst_cand", [P, max(k.chunks for k in EARLY)])
        worst_found = sb("worst_found", [P, 1])
        worst = sb("worst", [P, 2])
        too_many = sb("too_many", [P, 1])
        dense_needed = sb("dense_needed", [1, 1], I32)

        gathered = sb("gathered", [P, RING_SLOTS, 2 * D])
        q_tile = [sb(f"q_tile{b}", [P, D]) for b in range(2)]
        prod = scores[:, 0:MAX_SLOTS * D].rearrange("p (s d) -> p s d", d=D)
        ring = gathered[:].rearrange("p s d -> p (s d)")
        ring_rest, ring_second = ring[:, 0:EARLY_AT[1] * 2 * D], ring[:, EARLY_AT[1] * 2 * D:]
        adj_landing = ring_second.bitcast(I32)[:, 0:N]
        s_raw = sb("s_raw", [P, MAX_SLOTS, HEADS])
        s_msk = sb("s_msk", [P, MAX_SLOTS, HEADS])
        s_max = sb("s_max", [P, HEADS])
        s_sub = sb("s_sub", [P, MAX_SLOTS, HEADS])
        p_slot = sb("p_slot", [P, MAX_SLOTS, HEADS])
        p_sum = sb("p_sum", [P, HEADS])
        inv_sum = sb("inv_sum", [P, HEADS])
        attn = sb("attn", [P, D])

        x_tile = sb("x_tile", [P, D])
        attn_t = sb("attn_t", [P, P])
        x2 = [sb(f"x2_{b}", [P, D]) for b in range(2)]
        e_stat6 = sb("e_stat6", [P, 6])
        e_mean_var = sb("e_mean_var", [P, 2])
        e_std = sb("e_std", [P, 1])
        e_rstd = sb("e_rstd", [P, 1])
        x2_norm = sb("x2_norm", [P, D])
        h2_t = sb("h2_t", [P, P])
        gelu = mask_bias[:, 0:2 * FF].bitcast(F32)
        y_tile = sb("y_tile", [P, D])

        BANKS = 4
        ps_d = [psum(f"ps_d{b}") for b in range(BANKS)]
        ps_s, ps_t = ps_d[0:2], ps_d[2:4]
        ps_f, ps_attn, ps_proj, ps_norm = ps_d
        ps_o = psum("ps_o")
        ps_e = psum("ps_e")
        ps_c = psum("ps_c")
        ps_a = psum("ps_a")

        w_qkv_in = sem("w_qkv_in")
        norm_in = sem("norm_in")
        weights_in = sem("weights_in")
        ident_made = sem("ident_made")
        consts_made = sem("consts_made")
        const_step = sem("const_step")
        dve_past = sem("dve_past")
        pool_past = sem("pool_past")
        x_in = [sem("x_in0"), sem("x_in1")]
        p_stat6_made = sem("p_stat6_made")
        p_stats_made = sem("p_stats_made")
        p_std_made = sem("p_std_made")
        p_rstd_made = sem("p_rstd_made")
        p_norm_made = sem("p_norm_made")
        p_norm_turned = sem("p_norm_turned")
        p_h_made = sem("p_h_made")
        p_kv_ready = [sem("p_kv_ready0"), sem("p_kv_ready1")]
        p_kv_kept = [sem("p_kv_kept0"), sem("p_kv_kept1")]
        p_q_ready = sem("p_q_ready")
        p_q_kept = sem("p_q_kept")
        p_keys_ready = sem("p_keys_ready")
        p_keys_kept = sem("p_keys_kept")
        p_values_kept = sem("p_values_kept")
        kv_stored = [sem("kv_stored0"), sem("kv_stored1")]
        q_stored = [sem("q_stored0"), sem("q_stored1")]
        first_adj_in = sem("first_adj_in")
        adj_in = [sem("adj_in0"), sem("adj_in1")]
        squares_made = sem("squares_made")
        nonzero_made = sem("nonzero_made")
        codes_ready = sem("codes_ready")
        cands_found = sem("cands_found")
        cands_int = sem("cands_int")
        spread_made = sem("spread_made")
        round_found = sem("round_found")
        round_taken = sem("round_taken")
        found_read = sem("found_read")
        column_made = sem("column_made")
        index_made = sem("index_made")
        worst_step = sem("worst_step")
        kv_in = [sem(f"kv_in{q}") for q in range(DEPTH)]
        ring_clear = [sem("ring_clear0"), sem("ring_clear1")]
        q_in = [sem("q_in0"), sem("q_in1")]
        prod_made = sem("prod_made")
        s_raw_made = sem("s_raw_made")
        s_msk_made = sem("s_msk_made")
        s_max_made = sem("s_max_made")
        s_sub_made = sem("s_sub_made")
        p_made = sem("p_made")
        p_sum_made = sem("p_sum_made")
        weighted_first = sem("weighted_first")
        weighted_made = sem("weighted_made")
        inv_sum_made = sem("inv_sum_made")
        sum_ready = sem("sum_ready")
        attn_made = sem("attn_made")
        light_attn_made = sem("light_attn_made")
        d_adj_in = sem("d_adj_in")
        d_q_in = sem("d_q_in")
        d_bias_made = sem("d_bias_made")
        d_q_turned = sem("d_q_turned")
        d_q_kept = sem("d_q_kept")
        d_q_pack = sem("d_q_pack")
        d_scores_ready = sem("d_scores_ready")
        d_scores_masked = sem("d_scores_masked")
        d_row_max = sem("d_row_max")
        d_neg_max = sem("d_neg_max")
        d_probs_made = sem("d_probs_made")
        d_probs_turned = sem("d_probs_turned")
        d_turned_kept = [sem("d_turned_kept0"), sem("d_turned_kept1")]
        d_out_ready = sem("d_out_ready")
        d_inv_sum = sem("d_inv_sum")
        d_packed = sem("d_packed")
        d_unpacked = sem("d_unpacked")
        d_attn_made = sem("d_attn_made")
        xt_in = sem("xt_in")
        e_attn_turned = sem("e_attn_turned")
        e_attn_t_kept = sem("e_attn_t_kept")
        e_proj_ready = sem("e_proj_ready")
        e_x2_made = sem("e_x2_made")
        e_stat6_made = sem("e_stat6_made")
        e_stats_made = sem("e_stats_made")
        e_std_made = sem("e_std_made")
        e_rstd_made = sem("e_rstd_made")
        e_norm_made = sem("e_norm_made")
        e_norm_turned = sem("e_norm_turned")
        e_h2_made = sem("e_h2_made")
        e_ff1_ready = sem("e_ff1_ready")
        e_gelu_made = sem("e_gelu_made")
        e_ff2_ready = sem("e_ff2_ready")
        e_y_made = sem("e_y_made")
        y_stored = sem("y_stored")
        flag_summed = sem("flag_summed")
        flag_made = sem("flag_made")

        WEIGHT_LOADS = 3 + 3
        CONSTS = 12
        WIDE_TILES = sum(k.slots > 16 for k in EARLY)
        FIRST_PARTS = GROUPS - 4
        PARTS = 4
        ACT_PARTS, ACT_COLS = PARTS - 1, N // 4
        HALF = GROUP // 2
        TURNS = TILES // GROUP
        AHEAD = 5
        SEEK = 2
        FIRST_STEADY = len(EARLY)
        ROUNDS = (TILES - AHEAD - FIRST_STEADY) // DEPTH
        LAST_STEADY = FIRST_STEADY + DEPTH * ROUNDS
        assert FIRST_STEADY % DEPTH == 0

        x_tiles = x.rearrange("(t p) d -> p t d", p=P)
        q_tiles = q_dram.rearrange("(t p) d -> p t d", p=P)
        adj_tiles = adj.rearrange("(t p) n -> p t n", p=P)
        adj_rows = adj.rearrange("(t p) n -> p t n", p=HEAVY)
        out_tiles = out.rearrange("(t p) d -> p t d", p=P)

        def one(tiles, t):
            return tiles[:, bass.ds(t, 1), :].rearrange("p a n -> p (a n)")

        def count_before(s, what):
            if isinstance(s, int):
                return sum(what(kind_of(i)) for i in range(s))
            return what(NARROW) * (s - FIRST_STEADY) + sum(what(k) for k in EARLY)

        def chunks_of(kind):
            return kind.chunks

        def rounds_of(kind):
            return kind.rounds

        def takes_of(kind):
            return kind.rounds - 1

        def there(s, ahead):
            return not isinstance(s, int) or s + ahead < TILES

        def wait_adjacency(engine, s, b, r):
            if isinstance(s, int) and s == 0:
                engine.wait_ge(first_adj_in, 16 * FIRST_PARTS)
            else:
                engine.wait_ge(adj_in[b], 16 * (r + b))

        def is_early(s, n):
            return isinstance(s, int) and s < n

        def steady(engine, step):
            for s in range(FIRST_STEADY):
                step(s, s % 2, s // 2, 0, s % DEPTH)
            with engine.Fori(0, ROUNDS) as i:
                for q in range(DEPTH):
                    step(DEPTH * i + (FIRST_STEADY + q), q % 2, (DEPTH // 2) * i + (FIRST_STEADY + q) // 2, i, q)
            for s in range(LAST_STEADY, TILES):
                step(s, s % 2, s // 2, 0, s % DEPTH)

        block = ctx.enter_context(nc.Block())

        @block.sync
        def _(sp):
            x_groups = x.rearrange("(g t p) d -> g p t d", t=GROUP, p=P)
            kv_groups = kv_dram.rearrange("(g t p) d -> g p t d", t=GROUP, p=P)
            q_groups = q_dram.rearrange("(g t p) d -> g p t d", t=GROUP, p=P)

            def group(of, g):
                return of[bass.ds(g, 1)].rearrange("a p t d -> p (a t) d")

            sp.dma_start(x_grp[0], x_groups[0]).then_inc(x_in[0], 16)
            sp.dma_start(w_qkv_sb[:], w_qkv).then_inc(w_qkv_in, 16)
            sp.dma_start(x_grp[1], x_groups[1]).then_inc(x_in[1], 16)
            for i, v in enumerate((g1, be1, g2, be2)):
                sp.dma_start(norm_cols[:, i:i + 1], v.rearrange("(p a) -> p a", a=1)).then_inc(norm_in, 16)
            sp.dma_start(w_proj_sb[:], w_proj).then_inc(weights_in, 16)
            sp.dma_start(w1_sb[:], w1).then_inc(weights_in, 16)
            sp.dma_start(w2_sb[:], w2.rearrange("(b p) d -> p b d", p=P)).then_inc(weights_in, 16)
            sp.dma_start(bias_rows[:, 0:D], b_proj.rearrange("(a d) -> a d", a=1)).then_inc(weights_in, 16)
            sp.dma_start(bias_rows[:, D:2 * D], b2.rearrange("(a d) -> a d", a=1)).then_inc(weights_in, 16)
            sp.dma_start(b1_blocks[:], b1.rearrange("(f p) -> f p", p=P)).then_inc(weights_in, 16)
            def load_packed(rows):
                for j in range(HEADS):
                    sp.dma_start(adj_landing[j * HEAVY:(j + 1) * HEAVY, :], rows).then_inc(d_adj_in, 16)

            sp.wait_ge(p_norm_made, 1)
            sp.dma_start(x_grp[0], x_groups[2]).then_inc(x_in[0], 16)

            def project_pair(i, loads):
                for b in range(2):
                    g = 2 * i + b
                    if b < loads:
                        sp.wait_ge(p_norm_made, g + 2)
                        sp.dma_start(x_grp[1 - b], group(x_groups, g + 3)).then_inc(x_in[1 - b], 16)
                    if loads == 2:
                        part = bass.ds(g * (N // FIRST_PARTS), N // FIRST_PARTS)
                        sp.dma_start(adj_sb[0][:, part], adj[tile_of(0) * P:(tile_of(0) + 1) * P, part]
                                     ).then_inc(first_adj_in, 16)
                    sp.wait_ge(p_kv_kept[0], g + 1)
                    sp.wait_ge(p_kv_kept[1], g + 1)
                    sp.dma_start(group(kv_groups, g), kv_stage[b]).then_inc(kv_stored[b], 16)
                    sp.wait_ge(p_q_kept, g + 1)
                    sp.dma_start(group(q_groups, g), q_stage[b].rearrange("p (t d) -> p t d", t=GROUP)
                                 ).then_inc(q_stored[b], 16)

            with sp.Fori(0, FIRST_PARTS // 2) as i:
                project_pair(i, 2)
            project_pair(FIRST_PARTS // 2, 1)
            sp.wait_ge(q_stored[0], 16 * (GROUPS // 2 - 1))
            sp.dma_start(q_rows_d[:], q_dram[0:P, :]).then_inc(d_q_in, 16)
            project_pair(GROUPS // 2 - 1, 0)
            load_packed(adj[0:HEAVY, :])
            sp.dma_start(adj_sb[1][:], one(adj_tiles, tile_of(1))).then_inc(adj_in[1], 16)

            for b in range(2):
                sp.wait_ge(q_stored[b], 16 * (GROUPS // 2))
                sp.wait_ge(kv_stored[b], 16 * (GROUPS // 2))
            for s in range(2):
                sp.dma_start(q_tile[s][:], one(q_tiles, tile_of(s))).then_inc(q_in[s], 16)

            def load_adjacency(s, b):
                sp.wait_ge(nonzero_made, PARTS * (s - 1))
                sp.dma_start(adj_sb[b][:], one(adj_tiles, tile_of(s))).then_inc(adj_in[b], 16)

            for s in range(2, AHEAD):
                load_adjacency(s, s % 2)

            def load_x(n, t):
                if not is_early(n, 1):
                    sp.wait_ge(e_x2_made, n)
                sp.dma_start(x_tile[:], one(x_tiles, t)).then_inc(xt_in, 16)

            def store(n, t):
                sp.wait_ge(e_y_made, n + 1)
                sp.dma_start(one(out_tiles, t), y_tile[:]).then_inc(y_stored, 16)

            def step(s, b, r, i, q):
                if there(s, AHEAD):
                    load_adjacency(s + AHEAD, 1 - b)
                load_x(s, tile_of(s))
                if there(s, 2):
                    sp.wait_ge(prod_made, s + 1)
                    sp.dma_start(q_tile[b][:], one(q_tiles, tile_of(s + 2))).then_inc(q_in[b], 16)
                if not is_early(s, 3):
                    store(s - 3, tile_of(s - 3))

            steady(sp, step)
            for n in range(TILES - 3, TILES):
                store(n, n)
            sp.wait_ge(y_stored, 16 * TILES)
            sp.wait_ge(flag_made, 1)
            with sp.If(sp.value_load(dense_needed[0:1, 0:1], min_val=0, max_val=P) > 0):
                with sp.Fori(0, TILES) as t:
                    sp.wait_ge(d_q_turned, t + 1)
                    sp.dma_start(q_rows_d[:], one(q_tiles, t)).then_inc(d_q_in, 16)
                    for i in range(PARTS_OF_TILE):
                        sp.wait_ge(d_bias_made, t * PARTS_OF_TILE + (i + 1))
                        load_packed(adj_rows[:, bass.ds(t * PARTS_OF_TILE + i, 1), :].rearrange("p a n -> p (a n)"))
                    load_x(TILES + t, t)
                    store(TILES + t, t)
                sp.wait_ge(y_stored, 16 * 2 * TILES)

        @block.gpsimd
        def _(pool):
            nc.gpsimd.memset(ident[:], 0.0).then_inc(const_step, 1)
            nc.gpsimd.memset(zero_col[:], 0.0).then_inc(ident_made, 1)
            nc.gpsimd.memset(eps_col[:], EPS).then_inc(ident_made, 1)
            pool.wait_ge(const_step, 1)
            nc.gpsimd.affine_select(out=ident[:], in_=ident[:], compare_op=ALU.not_equal, fill=1.0, base=0,
                                    pattern=[[-1, P]], channel_multiplier=1).then_inc(ident_made, 1)
            nc.gpsimd.memset(head_mask[:], 1.0).then_inc(const_step, 1)
            nc.gpsimd.memset(pack_mask[:], 1.0).then_inc(const_step, 1)
            nc.gpsimd.memset(block_cols[:].rearrange("f c p -> f (c p)"), 0.0).then_inc(const_step, 1)
            nc.gpsimd.memset(light_rows[:], 1.0).then_inc(const_step, 1)
            nc.gpsimd.memset(fold_weights[:].rearrange("p k q -> p (k q)"), 0.0).then_inc(const_step, 1)
            nc.gpsimd.iota(position_low, [[0, 2], [1, BANK // 2]], base=0, channel_multiplier=0
                           ).then_inc(const_step, 1)
            nc.gpsimd.iota(position_high, [[BANK // 2, 2], [0, BANK // 2]], base=0, channel_multiplier=0
                           ).then_inc(const_step, 1)
            nc.gpsimd.memset(place[:], 0.0).then_inc(consts_made, 1)
            nc.gpsimd.memset(ones_row[:], 1.0).then_inc(consts_made, 1)
            nc.gpsimd.memset(ones_col[:], 1.0).then_inc(consts_made, 1)
            nc.gpsimd.memset(ones_bf[:], 1.0).then_inc(consts_made, 1)
            pool.wait_ge(const_step, 8)
            nc.gpsimd.affine_select(out=block_cols[:], in_=block_cols[:], compare_op=ALU.not_equal, fill=1.0, base=0,
                                    pattern=[[-1, FB], [0, P]], channel_multiplier=1).then_inc(consts_made, 1)
            for k in range(FOLDS):
                ins = nc.gpsimd.affine_select(out=fold_weights[:, k, :], in_=fold_weights[:, k, :],
                                              compare_op=ALU.not_equal, fill=float(BANK << k), base=0,
                                              pattern=[[-1, P]], channel_multiplier=1)
            ins.then_inc(consts_made, 1)
            nc.gpsimd.tensor_copy(position[:, 0, :], position_low).then_inc(consts_made, 1)
            nc.gpsimd.tensor_copy(position[:, 1, :], position_high).then_inc(consts_made, 1)
            for k in range(FOLDS):
                ins = nc.gpsimd.memset(fold_bit[:, k:k + 1], (BANK << k) + BANK - 1)
            ins.then_inc(consts_made, 1)
            nc.gpsimd.affine_select(out=head_mask[:], in_=head_mask[:], compare_op=ALU.is_ge, fill=0.0, base=0,
                                    pattern=[[-HD, HEADS]], channel_multiplier=1).then_inc(const_step, 1)
            nc.gpsimd.affine_select(out=pack_mask[:], in_=pack_mask[:], compare_op=ALU.is_ge, fill=0.0, base=0,
                                    pattern=[[-HEAVY, HEADS]], channel_multiplier=1).then_inc(const_step, 1)
            nc.gpsimd.affine_select(out=light_rows[:], in_=light_rows[:], compare_op=ALU.is_ge, fill=0.0, base=-HEAVY,
                                    pattern=[[0, 1]], channel_multiplier=1).then_inc(consts_made, 1)
            pool.wait_ge(const_step, 10)
            nc.gpsimd.affine_select(out=pack_mask[:], in_=pack_mask[:], compare_op=ALU.is_ge, fill=0.0, base=HEAVY - 1,
                                    pattern=[[HEAVY, HEADS]], channel_multiplier=-1).then_inc(consts_made, 1)
            nc.gpsimd.affine_select(out=head_mask[:], in_=head_mask[:], compare_op=ALU.is_ge, fill=0.0, base=HD - 1,
                                    pattern=[[HD, HEADS]], channel_multiplier=-1).then_inc(consts_made, 1)
            nc.gpsimd.memset(ring_rest, 0.0).then_inc(ring_clear[0], 1)

            def project_pair(i):
                for b in range(2):
                    g = 2 * i + b
                    pool.wait_ge(p_kv_kept[0], g + 1)
                    pool.wait_ge(p_kv_kept[1], g + 1)
                    pool.sem_inc(pool_past, 1)
                    nc.gpsimd.tensor_copy(values[:, bass.ds(g * GROUP, GROUP), :], kv_stage[b][:, :, D:2 * D]
                                          ).then_inc(p_values_kept, 1)

            with pool.Fori(0, GROUPS // 2) as i:
                project_pair(i)

            for b in range(2):
                pool.wait_ge(kv_stored[b], 16 * (GROUPS // 2))
            def gather(s, b, r, i, q):
                pool.wait_ge(index_made, s + 1)
                if is_early(s, 2):
                    pool.wait_ge(ring_clear[b], 1)
                waited = 0
                if not isinstance(s, int):
                    pool.wait_ge(weighted_made, weighed_before(s))
                    pool.sem_inc(pool_past, 1)
                for j in range(kind_of(s).slots):
                    if isinstance(s, int) and last_in_slot(s, j) > waited:
                        waited = last_in_slot(s, j)
                        pool.wait_ge(weighted_made, waited)
                        pool.sem_inc(pool_past, 1)
                    pool.indirect_dma_start(gathered[:, slots_in_ring(s, q).start + j, :], None, kv_dram,
                                            bass.IndirectOffsetOnAxis(ap=index[q][:, j:j + 1], axis=0),
                                            bounds_check=N - 1, oob_is_err=False).then_inc(kv_in[q], 16)

            steady(pool, gather)

        @block.tensor
        def _(pe):
            pe.wait_ge(ident_made, 3)
            pe.wait_ge(w_qkv_in, 16)

            def turn_group(g, b):
                pe.wait_ge(p_norm_made, g + 1)
                for t in range(GROUP):
                    mm = nc.tensor.transpose(ps_s[b][:, t * P:(t + 1) * P], x_nrm[b][:, t, :], ident[:])
                mm.then_inc(p_norm_turned, 1)

            def project_pair(i, first=False, last=False):
                for b in range(2):
                    g = 2 * i + b
                    pe.wait_ge(p_h_made, g + 1)
                    for half in range(2):
                        if not (first and b == 0):
                            pe.wait_ge(p_kv_kept[half], g)
                        for u in range(HALF):
                            t = half * HALF + u
                            mm = nc.tensor.matmul(ps_t[half][:, u * 2 * D:(u + 1) * 2 * D],
                                                  h_t[b][:, t * P:(t + 1) * P], w_qkv_sb[:, D:3 * D],
                                                  start=True, stop=True)
                        mm.then_inc(p_kv_ready[half], 1)
                        if half == 0 and not (last and b == 1):
                            turn_group(g + 1, 1 - b)
                    if not (first and b == 0):
                        pe.wait_ge(p_q_kept, g)
                    for t in range(GROUP):
                        mm = nc.tensor.matmul(ps_o[:, t * P:(t + 1) * P], h_t[b][:, t * P:(t + 1) * P],
                                              w_qkv_sb[:, 0:D], start=True, stop=True)
                    mm.then_inc(p_q_ready, 1)
                    if not (first and b == 0):
                        pe.wait_ge(p_keys_kept, g)
                    nc.tensor.matmul(ps_e[:], w_qkv_sb[:, D:2 * D], h_t[b], start=True, stop=True
                                     ).then_inc(p_keys_ready, 1)

            turn_group(0, 0)
            project_pair(0, first=True)
            pe.wait_ge(consts_made, CONSTS)
            pe.wait_ge(weights_in, 16 * WEIGHT_LOADS)
            with pe.Fori(1, GROUPS // 2 - 1) as i:
                project_pair(i)
            project_pair(GROUPS // 2 - 1, last=True)
            for half in range(2):
                pe.wait_ge(p_kv_kept[half], GROUPS)
            pe.wait_ge(p_q_kept, GROUPS)
            pe.wait_ge(p_keys_kept, GROUPS)

            def codes(s):
                pe.wait_ge(nonzero_made, PARTS * (s + 1))
                if not is_early(s, 1):
                    pe.wait_ge(cands_found, count_before(s, chunks_of))
                for k in range(FOLDS):
                    nc.tensor.matmul(ps_c[:], fold_weights[:, k, :], nonzero[:, k * BANK:(k + 1) * BANK],
                                     start=(k == 0), stop=False)
                for a in range(2):
                    mm = nc.tensor.matmul(ps_c[:], ones_bf[:], position[:, a, :], start=False, stop=(a == 1))
                mm.then_inc(codes_ready, 1)

            def sum_slots(s):
                wide = is_early(s, WIDE_TILES)
                if wide:
                    pe.wait_ge(weighted_first, s + 1)
                else:
                    pe.wait_ge(weighted_made, s + 1)
                if not is_early(s, 1):
                    pe.wait_ge(attn_made, s)
                else:
                    pe.wait_ge(d_attn_made, 1)
                slots = kind_of(s).slots
                for j in range(slots):
                    if wide and j == slots // 2:
                        pe.wait_ge(weighted_made, s + 1)
                    mm = nc.tensor.matmul(ps_a[:, 0:D], ident[:], prod[:, j, :],
                                          start=(j == 0), stop=(j == slots - 1))
                mm.then_inc(sum_ready, 1)

            def tail_turn(n, rows):
                if rows is attn:
                    pe.wait_ge(attn_made, n + 1)
                nc.tensor.transpose(ps_attn[:, 0:P], rows[:], ident[:]).then_inc(e_attn_turned, 1)

            def tail_project(n):
                pe.wait_ge(e_attn_t_kept, n + 1)
                if not is_early(n, 1):
                    pe.wait_ge(e_x2_made, n)
                nc.tensor.matmul(ps_proj[:, 0:P], attn_t[:], w_proj_sb[:], start=True, stop=False)
                nc.tensor.matmul(ps_proj[:, 0:P], ones_row[:], bias_rows[:, 0:D], start=False, stop=True
                                 ).then_inc(e_proj_ready, 1)

            def tail_turn_norm(n):
                pe.wait_ge(e_norm_made, n + 1)
                nc.tensor.transpose(ps_norm[:, 0:P], x2_norm[:], ident[:]).then_inc(e_norm_turned, 1)

            def tail_feed(n):
                pe.wait_ge(e_h2_made, n + 1)
                if not is_early(n, 1):
                    pe.wait_ge(e_gelu_made, n)
                nc.tensor.matmul(ps_f[:], b1_blocks[:], block_cols[:].rearrange("f c p -> f (c p)"),
                                 start=True, stop=False)
                for f in range(FB):
                    mm = nc.tensor.matmul(ps_f[:, f * P:(f + 1) * P], w1_sb[:, f * P:(f + 1) * P], h2_t[:],
                                          start=False, stop=(f == FB - 1))
                mm.then_inc(e_ff1_ready, 1)

            def tail_out(n):
                pe.wait_ge(e_gelu_made, n + 1)
                if not is_early(n, 1):
                    pe.wait_ge(e_y_made, n)
                for f in range(FB):
                    nc.tensor.matmul(ps_e[:, 0:D], gelu[:, f * P:(f + 1) * P], w2_sb[:, f, :],
                                          start=(f == 0), stop=False)
                nc.tensor.matmul(ps_e[:, 0:D], ones_row[:], bias_rows[:, D:2 * D], start=False, stop=True
                                 ).then_inc(e_ff2_ready, 1)

            def dense_begin(n):
                pe.wait_ge(d_q_in, 16 * (n + 1))
                nc.tensor.transpose(ps_o[:, P:2 * P], q_rows_d[:], ident[:]).then_inc(d_q_turned, 1)

            def dense_scores(k, first=False):
                pe.wait_ge(d_q_pack, k + 1)
                for c in range(CHUNKS):
                    if c >= BANKS:
                        pe.wait_ge(d_scores_masked, k * CHUNKS + c - BANKS + 1)
                    nc.tensor.matmul(ps_d[c % BANKS][:], q_pack[:].rearrange("p j r -> p (j r)"),
                                     keys_t[:, c * BANK:(c + 1) * BANK], start=True, stop=True
                                     ).then_inc(d_scores_ready, 1)

            def dense_turn(k):
                pe.wait_ge(d_probs_made, k + 1)
                for j in range(TURNS):
                    if j >= BANKS:
                        pe.wait_ge(d_turned_kept[j % 2], k * (TURNS // 2) + (j - BANKS) // 2 + 1)
                    for u in range(GROUP):
                        c = j * GROUP + u
                        mm = nc.tensor.transpose(ps_d[j % BANKS][:, u * P:(u + 1) * P], scores[:, c * P:(c + 1) * P], ident[:])
                    mm.then_inc(d_probs_turned, 1)

            def dense_values(k):
                for j in range(2):
                    pe.wait_ge(d_turned_kept[j], (k + 1) * (TURNS // 2))
                if not is_early(k, 1):
                    pe.wait_ge(d_packed, k)
                for c in range(TILES):
                    mm = nc.tensor.matmul(ps_o[:, 0:D], probs_t[:, c, :], values[:, c, :],
                                          start=(c == 0), stop=(c == TILES - 1))
                mm.then_inc(d_out_ready, 1)

            def dense_unpack(k, i, last):
                pe.wait_ge(d_packed, k + 1)
                nc.tensor.matmul(ps_a[:, 0:D], place[:, PLACE - i * HEAVY:PLACE - i * HEAVY + P],
                                 packed.rearrange("p h d -> p (h d)"), start=(i == 0), stop=last
                                 ).then_inc(d_unpacked, 1)

            codes(0)
            dense_begin(0)
            dense_scores(0)
            codes(1)
            dense_turn(0)
            pe.wait_ge(p_values_kept, GROUPS)
            pe.wait_ge(consts_made, CONSTS + 1)
            codes(2)
            dense_values(0)
            dense_unpack(0, 0, True)

            def step(s, b, r, i, q):
                if not is_early(s, 1):
                    sum_slots(s - 1)
                if not is_early(s, 2):
                    tail_turn_norm(s - 2)
                if not is_early(s, 1):
                    tail_turn(s - 1, attn)
                if not is_early(s, 2):
                    tail_feed(s - 2)
                if not is_early(s, 1):
                    tail_project(s - 1)
                if there(s, 3):
                    codes(s + 3)
                if not is_early(s, 2):
                    tail_out(s - 2)

            steady(pe, step)
            sum_slots(TILES - 1)
            tail_turn_norm(TILES - 2)
            tail_turn(TILES - 1, attn)
            tail_project(TILES - 1)
            tail_feed(TILES - 2)
            tail_turn_norm(TILES - 1)
            tail_out(TILES - 2)
            tail_feed(TILES - 1)
            pe.wait_ge(flag_summed, 1)
            nc.tensor.matmul(ps_c[0:1, 0:1], too_many[:], ones_col[:], start=True, stop=True).then_inc(flag_summed, 1)
            tail_out(TILES - 1)


            pe.wait_ge(flag_made, 1)
            with pe.If(pe.value_load(dense_needed[0:1, 0:1], min_val=0, max_val=P) > 0):
                with pe.Fori(0, TILES) as t:
                    pe.wait_ge(e_y_made, t + TILES)
                    dense_begin(t + 1)
                    for i in range(PARTS_OF_TILE):
                        k = t * PARTS_OF_TILE + (i + 1)
                        dense_scores(k)
                        dense_turn(k)
                        dense_values(k)
                        dense_unpack(k, i, i == PARTS_OF_TILE - 1)
                    pe.wait_ge(d_attn_made, t + 2)
                    tail_turn(TILES + t, attn_d)
                    tail_project(TILES + t)
                    tail_turn_norm(TILES + t)
                    tail_feed(TILES + t)
                    tail_out(TILES + t)

        @block.scalar
        def _(act):
            act.wait_ge(ident_made, 3)

            def deviation(g, b):
                act.wait_ge(p_stats_made, g + 1)
                nc.scalar.activation(std[b][:], mean_var[b][:, :, 1], ACT.Sqrt, bias=eps_col[:]).then_inc(p_std_made, 1)

            def scale_group(g, b):
                act.wait_ge(p_norm_turned, g + 1)
                nc.scalar.activation(h_t[b], ps_s[b][:], ACT.Identity, bias=norm_cols[:, 1:2],
                                     scale=norm_cols[:, 0:1]).then_inc(p_h_made, 1)

            def part_of(b, q):
                cols = slice(q * ACT_COLS, (q + 1) * ACT_COLS)
                entries = adj_sb[b][:, cols]
                return entries, entries.bitcast(BF16)[:, 0:ACT_COLS], nonzero[:, cols]

            def square(s, b, r, q):
                if q == 0:
                    wait_adjacency(act, s, b, r)
                entries, squares, _ = part_of(b, q)
                nc.scalar.activation(squares, entries, ACT.Square).then_inc(squares_made, 1)

            def sign(s, b, q):
                act.wait_ge(squares_made, ACT_PARTS * s + q + 1)
                if q == 0 and not is_early(s, 1):
                    act.wait_ge(codes_ready, s)
                _, squares, marks = part_of(b, q)
                nc.scalar.activation(marks, squares, ACT.Sign).then_inc(nonzero_made, 1)

            def square_all(s):
                for q in range(ACT_PARTS):
                    square(s, s % 2, s // 2, q)

            def sign_all(s):
                for q in range(ACT_PARTS):
                    sign(s, s % 2, q)

            def project_pair(i, last=False):
                for b in range(2):
                    g = 2 * i + b
                    if not (last and b == 1):
                        scale_group(g + 1, 1 - b)
                    if not last:
                        deviation(g + 2, b)
                    else:
                        square(0, 0, 0, 2 * b)
                    act.wait_ge(p_kv_ready[1], g + 1)
                    if not (isinstance(i, int) and i == 0):
                        act.wait_ge(kv_stored[b], 16 * i)
                        act.wait_ge(p_values_kept, g - 1)
                    nc.scalar.copy(kv_stage[b][:, HALF:, :].rearrange("p t d -> p (t d)"), ps_t[1][:]
                                   ).then_inc(p_kv_kept[1], 1)
                    if last:
                        if b == 0:
                            square(0, 0, 0, 1)
                        sign(0, 0, b)
                    act.wait_ge(p_keys_ready, g + 1)
                    nc.scalar.copy(keys_t[:, bass.ds(g * BANK, BANK)], ps_e[:]).then_inc(p_keys_kept, 1)

            deviation(0, 0)
            deviation(1, 1)
            act.wait_ge(norm_in, 16 * 4)
            scale_group(0, 0)
            project_pair(0)
            with act.Fori(1, GROUPS // 2 - 1) as i:
                project_pair(i)
            project_pair(GROUPS // 2 - 1, True)

            def tail_turned(n):
                act.wait_ge(e_attn_turned, n + 1)
                nc.scalar.copy(attn_t[:], ps_attn[:, 0:P]).then_inc(e_attn_t_kept, 1)

            def tail_std(n):
                act.wait_ge(e_stats_made, n + 1)
                nc.scalar.activation(e_std[:], e_mean_var[:, 1:2], ACT.Sqrt, bias=eps_col[:]).then_inc(e_std_made, 1)

            def tail_h2(n):
                act.wait_ge(e_norm_turned, n + 1)
                nc.scalar.activation(h2_t[:], ps_norm[:, 0:P], ACT.Identity, bias=norm_cols[:, 3:4],
                                     scale=norm_cols[:, 2:3]).then_inc(e_h2_made, 1)

            def tail_gelu(n):
                act.wait_ge(e_ff1_ready, n + 1)
                nc.scalar.activation(gelu[:], ps_f[:], ACT.Gelu_apprx_tanh).then_inc(e_gelu_made, 1)

            def dense_begin(n):
                act.wait_ge(d_q_turned, n + 1)
                nc.scalar.copy(q_t[:], ps_o[:, P:2 * P]).then_inc(d_q_kept, 1)

            def dense_exp(k):
                act.wait_ge(d_neg_max, k + 1)
                nc.scalar.activation(scores[:], scores[:], ACT.Exp, bias=neg_max[:], scale=SCALE,
                                     accum_out=row_sum[:]).then_inc(d_probs_made, 1)

            def dense_keep(k, j):
                act.wait_ge(d_probs_turned, k * TURNS + j + 1)
                nc.scalar.copy(probs_t[:, j * GROUP:(j + 1) * GROUP, :].rearrange("p a b -> p (a b)"),
                               ps_d[j % BANKS][:]).then_inc(d_turned_kept[0], 1)

            sign(0, 0, 2)
            dense_begin(0)
            square_all(1)
            sign_all(1)
            act.wait_ge(d_bias_made, 1)
            nc.scalar.copy(ring_second, zero_col[:].broadcast_to([P, (RING_SLOTS - EARLY_AT[1]) * 2 * D])
                           ).then_inc(ring_clear[1], 1)
            dense_exp(0)
            for b in range(2):
                act.wait_ge(kv_stored[b], 16 * (GROUPS // 2))
            act.wait_ge(p_values_kept, GROUPS)
            square_all(2)
            for n, j in enumerate(range(0, TURNS, 2)):
                dense_keep(0, j)
                if n < ACT_PARTS:
                    sign(2, 0, n)
            square_all(3)

            def step(s, b, r, i, q):
                if there(s, 3):
                    for part in range(ACT_PARTS):
                        sign(s + 3, 1 - b, part)
                if not is_early(s, 2):
                    tail_h2(s - 2)
                if not is_early(s, 1):
                    tail_turned(s - 1)
                if there(s, 4):
                    for part in range(1):
                        square(s + 4, b, r + 2, part)
                if not is_early(s, 2):
                    tail_gelu(s - 2)
                act.wait_ge(s_sub_made, s + 1)
                slots = kind_of(s).slots
                nc.scalar.activation(p_slot[:, 0:slots, :], s_sub[:, 0:slots, :], ACT.Exp, scale=SCALE
                                     ).then_inc(p_made, 1)
                if not is_early(s, 1):
                    tail_std(s - 1)
                if there(s, 4):
                    for part in range(1, ACT_PARTS):
                        square(s + 4, b, r + 2, part)

            steady(act, step)
            tail_h2(TILES - 2)
            tail_turned(TILES - 1)
            tail_std(TILES - 1)
            tail_gelu(TILES - 2)
            tail_h2(TILES - 1)
            tail_gelu(TILES - 1)
            act.wait_ge(flag_made, 1)
            with act.If(act.value_load(dense_needed[0:1, 0:1], min_val=0, max_val=P) > 0):
                with act.Fori(0, TILES) as t:
                    act.wait_ge(d_q_pack, t * PARTS_OF_TILE + 1)
                    dense_begin(t + 1)
                    for i in range(PARTS_OF_TILE):
                        k = t * PARTS_OF_TILE + (i + 1)
                        dense_exp(k)
                        for j in range(0, TURNS, 2):
                            dense_keep(k, j)
                    tail_turned(TILES + t)
                    tail_std(TILES + t)
                    tail_h2(TILES + t)
                    tail_gelu(TILES + t)

        @block.vector
        def _(dve):
            nc.vector.memset(worst_cand[:], 0.0).then_inc(worst_step, 1)
            nc.vector.memset(worst_found[:], 0.0).then_inc(worst_step, 1)

            def dense_mask(n):
                dve.wait_ge(d_adj_in, 16 * HEADS * (n + 1))
                nc.vector.tensor_scalar(mask_bias[:], adj_landing, 0.0, MASKED, ALU.is_equal, ALU.mult
                                        ).then_inc(d_bias_made, 1)

            def statistics(g, b, r):
                dve.wait_ge(x_in[b], 16 * (r + 1))
                for t in range(GROUP):
                    ins = nc.vector.bn_stats(stat6[b][:, t, :], x_grp[b][:, t, :])
                ins.then_inc(p_stat6_made, 1)
                dve.wait_ge(p_stat6_made, g + 1)
                dve.sem_inc(dve_past, 1)
                for t in range(GROUP):
                    ins = nc.vector.bn_aggr(mean_var[b][:, t, :], stat6[b][:, t, :])
                ins.then_inc(p_stats_made, 1)

            def keep(g, b, r, first):
                dve.wait_ge(p_kv_ready[0], g + 1)
                if not first:
                    dve.wait_ge(kv_stored[b], 16 * r)
                    dve.wait_ge(p_values_kept, g - 1)
                nc.vector.tensor_copy(kv_stage[b][:, 0:HALF, :].rearrange("p t d -> p (t d)"), ps_t[0][:]
                                      ).then_inc(p_kv_kept[0], 1)
                dve.wait_ge(p_q_ready, g + 1)
                if not first:
                    dve.wait_ge(q_stored[b], 16 * r)
                nc.vector.tensor_copy(q_stage[b], ps_o[:]).then_inc(p_q_kept, 1)

            def mark(s, b, r):
                cols = slice(ACT_PARTS * ACT_COLS, N)
                wait_adjacency(dve, s, b, r)
                if not is_early(s, 1):
                    dve.wait_ge(codes_ready, s)
                nc.vector.tensor_scalar(nonzero[:, cols], adj_sb[b][:, cols], 0.0, None, ALU.not_equal
                                        ).then_inc(nonzero_made, 1)

            def normalise(g, b, first=False):
                dve.wait_ge(p_std_made, g + 1)
                nc.vector.reciprocal(rstd[b][:], std[b][:]).then_inc(p_rstd_made, 1)
                dve.wait_ge(p_rstd_made, g + 1)
                if not first:
                    dve.wait_ge(p_norm_turned, g - 1)
                for t in range(GROUP):
                    ins = nc.vector.tensor_scalar(x_nrm[b][:, t, :], x_grp[b][:, t, :], mean_var[b][:, t, 0:1],
                                                  rstd[b][:, t:t + 1], ALU.subtract, ALU.mult)
                ins.then_inc(p_norm_made, 1)

            def project_pair(i, last=False):
                first = isinstance(i, int) and i == 0
                for b in range(2):
                    g = 2 * i + b
                    if not (last and b == 1):
                        normalise(g + 1, 1 - b, first and b == 0)
                    if not last:
                        statistics(g + 2, b, i + 1)
                    elif b == 0:
                        mark(0, 0, 0)
                    keep(g, b, i, first)

            statistics(0, 0, 0)
            statistics(1, 1, 0)
            normalise(0, 0, True)
            project_pair(0)
            dve.wait_ge(consts_made, CONSTS)
            nc.vector.tensor_reduce(place[:, PLACE:P], ident[:].rearrange("p (h r) -> p r h", h=HEADS), AX.X, ALU.add
                                    ).then_inc(consts_made, 1)
            with dve.Fori(1, GROUPS // 2 - 1) as i:
                project_pair(i)
            project_pair(GROUPS // 2 - 1, True)

            def candidates(s):
                kind = kind_of(s)
                dve.wait_ge(codes_ready, s + 1)
                dve.sem_inc(dve_past, 1)
                for c in range(kind.chunks):
                    nc.vector.max(cand[:, 8 * c:8 * c + 8], ps_c[:, c::kind.chunks]).then_inc(cands_found, 1)

            def candidates_int(s):
                kind = kind_of(s)
                dve.wait_ge(cands_found, count_before(s, chunks_of) + kind.chunks)
                nc.vector.tensor_copy(cand_int[:, 0:kind.cands], cand[:, 0:kind.cands]).then_inc(cands_int, 1)

            def spread_folds(s):
                kind = kind_of(s)
                dve.wait_ge(cands_int, s + 1)
                nc.vector.tensor_tensor(spread[:, 0:kind.cands, :],
                                        cand_int[:, 0:kind.cands].unsqueeze(2).broadcast_to([P, kind.cands, FOLDS]),
                                        fold_bit[:].unsqueeze(1).broadcast_to([P, kind.cands, FOLDS]), ALU.bitwise_and).then_inc(spread_made, 1)

            def note_candidates(s):
                kind = kind_of(s)
                dve.wait_ge(worst_step, 2 * (s + 1))
                if is_heavy(s):
                    nc.vector.scalar_tensor_tensor(worst_cand[:, 0:kind.chunks], cand[:, 7:kind.cands:8], light_rows[:],
                                                   worst_cand[:, 0:kind.chunks], ALU.mult, ALU.max
                                                   ).then_inc(worst_step, 1)
                    return
                nc.vector.tensor_tensor(worst_cand[:, 0:kind.chunks], worst_cand[:, 0:kind.chunks],
                                        cand[:, 7:kind.cands:8], ALU.max).then_inc(worst_step, 1)

            def sources(kind):
                flat = spread[:, 0:kind.cands, :].rearrange("p a b -> p (a b)")
                rest = spread_rest[:, 0:kind.cands * FOLDS]
                return [flat, rest, flat, rest]

            def find_round(s, r):
                kind = kind_of(s)
                if r == 0:
                    dve.wait_ge(spread_made, s + 1)
                else:
                    dve.wait_ge(round_taken, count_before(s, takes_of) + r)
                dve.sem_inc(dve_past, 1)
                nc.vector.max(found[:, 8 * r:8 * r + 8], sources(kind)[r]).then_inc(round_found, 1)

            def take_round(s, r):
                kind = kind_of(s)
                dve.wait_ge(round_found, count_before(s, rounds_of) + r + 1)
                dve.sem_inc(dve_past, 1)
                nc.vector.match_replace(sources(kind)[r + 1], found[:, 8 * r:8 * r + 8], sources(kind)[r], 0.0
                                        ).then_inc(round_taken, 1)

            def decode_bias(s, q):
                kind = kind_of(s)
                dve.wait_ge(round_found, count_before(s, rounds_of) + kind.rounds)
                nc.vector.tensor_scalar(slot_bias[q][:, 0:kind.slots], found[:, 0:kind.slots], float(BANK), MASKED,
                                        ALU.is_lt, ALU.mult).then_inc(found_read, 1)
                nc.vector.tensor_copy(found_int[:, 0:kind.slots], found[:, 0:kind.slots]).then_inc(found_read, 1)
                nc.vector.tensor_scalar(fold[:, 0:kind.slots], found[:, 0:kind.slots].bitcast(I32), 23, FOLDS - 1,
                                        ALU.logical_shift_right, ALU.bitwise_and).then_inc(found_read, 1)

            def decode_low(s):
                kind = kind_of(s)
                dve.wait_ge(found_read, 4 * s + 3)
                nc.vector.tensor_scalar(low[:, 0:kind.slots], found_int[:, 0:kind.slots], BANK - 1, None,
                                        ALU.bitwise_and).then_inc(found_read, 1)

            def decode_column(s):
                kind = kind_of(s)
                dve.wait_ge(found_read, 4 * (s + 1))
                nc.vector.scalar_tensor_tensor(column[:, 0:kind.slots], fold[:, 0:kind.slots], float(BANK),
                                               low[:, 0:kind.slots], ALU.mult, ALU.add).then_inc(column_made, 1)

            def decode_index(s, q):
                kind = kind_of(s)
                dve.wait_ge(column_made, s + 1)
                nc.vector.scalar_tensor_tensor(index[q][:, 0:kind.slots], slot_bias[q][:, 0:kind.slots], FAR / MASKED,
                                               column[:, 0:kind.slots], ALU.mult, ALU.add).then_inc(index_made, 1)

            def note_found(s):
                kind = kind_of(s)
                dve.wait_ge(worst_step, 2 * (s + 1) + 1)
                if is_heavy(s):
                    nc.vector.scalar_tensor_tensor(worst_found[:], found[:, kind.slots:kind.slots + 1], light_rows[:],
                                                   worst_found[:], ALU.mult, ALU.max).then_inc(worst_step, 1)
                    return
                nc.vector.tensor_tensor(worst_found[:], worst_found[:], found[:, kind.slots:kind.slots + 1],
                                        ALU.max).then_inc(worst_step, 1)

            def products(s, b, r, i, q):
                slots = kind_of(s).slots
                dve.wait_ge(kv_in[q], 16 * gathers_until(s, i, q))
                dve.wait_ge(q_in[b], 16 * (r + 1))
                if not is_early(s, 1):
                    dve.wait_ge(sum_ready, s)
                nc.vector.tensor_tensor(prod[:, 0:slots, :], gathered[:, slots_in_ring(s, q), 0:D],
                                        q_tile[b][:].unsqueeze(1).broadcast_to([P, slots, D]), ALU.mult
                                        ).then_inc(prod_made, 1)

            def scores_of_slots(s):
                slots = kind_of(s).slots
                dve.wait_ge(prod_made, s + 1)
                nc.vector.tensor_reduce(s_raw[:, 0:slots, :].rearrange("p s h -> p (s h)"),
                                        prod[:, 0:slots, :].rearrange("p s (h d) -> p (s h) d", d=HD), AX.X, ALU.add
                                        ).then_inc(s_raw_made, 1)

            def mask_slots(s, q):
                slots = kind_of(s).slots
                dve.wait_ge(s_raw_made, s + 1)
                nc.vector.tensor_tensor(s_msk[:, 0:slots, :], s_raw[:, 0:slots, :],
                                        slot_bias[q][:, 0:slots].unsqueeze(2).broadcast_to([P, slots, HEADS]), ALU.add
                                        ).then_inc(s_msk_made, 1)

            def max_slots(s):
                slots = kind_of(s).slots
                dve.wait_ge(s_msk_made, s + 1)
                nc.vector.tensor_reduce(s_max[:], s_msk[:, 0:slots, :].rearrange("p s h -> p h s"), AX.X, ALU.max
                                        ).then_inc(s_max_made, 1)

            def subtract_max(s):
                slots = kind_of(s).slots
                dve.wait_ge(s_max_made, s + 1)
                nc.vector.tensor_tensor(s_sub[:, 0:slots, :], s_msk[:, 0:slots, :],
                                        s_max[:].unsqueeze(1).broadcast_to([P, slots, HEADS]), ALU.subtract
                                        ).then_inc(s_sub_made, 1)

            def weigh_values(s, b, q):
                slots = kind_of(s).slots
                dve.wait_ge(p_made, s + 1)
                nc.vector.tensor_reduce(p_sum[:], p_slot[:, 0:slots, :].rearrange("p s h -> p h s"), AX.X, ALU.add
                                        ).then_inc(p_sum_made, 1)
                at = slots_in_ring(s, q).start

                def weigh(first, last):
                    v = gathered[:, at + first:at + last, D:2 * D].rearrange("p s (h d) -> p s h d", d=HD)
                    weights = p_slot[:, first:last, :].unsqueeze(3).broadcast_to([P, last - first, HEADS, HD])
                    weighted = prod[:, first:last, :].rearrange("p s (h d) -> p s h d", d=HD)
                    return nc.vector.tensor_tensor(weighted, v, weights, ALU.mult)

                half = slots // 2 if is_early(s, WIDE_TILES) else 0
                if half:
                    weigh(0, half).then_inc(weighted_first, 1)
                weigh(half, slots).then_inc(weighted_made, 1)
                dve.wait_ge(p_sum_made, s + 1)
                nc.vector.reciprocal(inv_sum[:], p_sum[:]).then_inc(inv_sum_made, 1)

            def finish_attention(s):
                dve.wait_ge(inv_sum_made, s + 1)
                dve.wait_ge(sum_ready, s + 1)
                if not is_early(s, 1):
                    dve.wait_ge(e_attn_turned, s)
                ins = nc.vector.tensor_tensor(attn[:].rearrange("p (h d) -> p h d", d=HD),
                                              ps_a[:, 0:D].rearrange("p (h d) -> p h d", d=HD),
                                              inv_sum[:].unsqueeze(2).broadcast_to([P, HEADS, HD]), ALU.mult)
                if is_heavy(s):
                    ins.then_inc(light_attn_made, 1)
                    dve.wait_ge(light_attn_made, 1)
                    dve.wait_ge(d_attn_made, 1)
                    ins = nc.vector.tensor_copy(attn[0:HEAVY, :], attn_d[0:HEAVY, :])
                ins.then_inc(attn_made, 1)

            def tail_residual(n, b):
                dve.wait_ge(xt_in, 16 * (n + 1))
                dve.wait_ge(e_proj_ready, n + 1)
                nc.vector.tensor_tensor(x2[b][:], ps_proj[:, 0:P], x_tile[:], ALU.add).then_inc(e_x2_made, 1)

            def tail_stat6(n, b):
                dve.wait_ge(e_x2_made, n + 1)
                nc.vector.bn_stats(e_stat6[:], x2[b][:]).then_inc(e_stat6_made, 1)

            def tail_stats(n):
                dve.wait_ge(e_stat6_made, n + 1)
                dve.sem_inc(dve_past, 1)
                nc.vector.bn_aggr(e_mean_var[:], e_stat6[:]).then_inc(e_stats_made, 1)

            def tail_rstd(n):
                dve.wait_ge(e_std_made, n + 1)
                nc.vector.reciprocal(e_rstd[:], e_std[:]).then_inc(e_rstd_made, 1)

            def tail_norm(n, b):
                dve.wait_ge(e_rstd_made, n + 1)
                nc.vector.tensor_scalar(x2_norm[:], x2[b][:], e_mean_var[:, 0:1], e_rstd[:], ALU.subtract, ALU.mult
                                        ).then_inc(e_norm_made, 1)

            def tail_end(n, b):
                dve.wait_ge(e_ff2_ready, n + 1)
                if not is_early(n, 1):
                    dve.wait_ge(y_stored, 16 * n)
                nc.vector.tensor_tensor(y_tile[:], ps_e[:, 0:D], x2[b][:], ALU.add).then_inc(e_y_made, 1)

            def dense_scores(k, i, first=False):
                if not first:
                    dve.wait_ge(d_scores_ready, k * CHUNKS)
                nc.vector.tensor_tensor(q_pack[:], q_t[:, i * HEAVY:(i + 1) * HEAVY].unsqueeze(1).broadcast_to([P, HEADS, HEAVY]),
                                        head_mask[:].unsqueeze(2).broadcast_to([P, HEADS, HEAVY]),
                                        ALU.mult).then_inc(d_q_pack, 1)
                if not first:
                    dve.wait_ge(d_probs_turned, k * TURNS)
                    dve.sem_inc(dve_past, 1)
                for c in range(CHUNKS):
                    dve.wait_ge(d_scores_ready, k * CHUNKS + c + 1)
                    dve.sem_inc(dve_past, 1)
                    nc.vector.tensor_tensor_reduce(
                        scores[:, c * BANK:(c + 1) * BANK], ps_d[c % BANKS][:], mask_bias[:, c * BANK:(c + 1) * BANK],
                        1.0, MASKED, ALU.add, ALU.max, chunk_max[:, c:c + 1]).then_inc(d_scores_masked, 1)
                dve.wait_ge(d_scores_masked, (k + 1) * CHUNKS)
                nc.vector.tensor_reduce(row_max[:], chunk_max[:], AX.X, ALU.max).then_inc(d_row_max, 1)
                dve.wait_ge(d_row_max, k + 1)
                nc.vector.tensor_scalar(neg_max[:], row_max[:], -SCALE, None, ALU.mult).then_inc(d_neg_max, 1)

            def dense_keep(k):
                for j in range(1, TURNS, 2):
                    dve.wait_ge(d_probs_turned, k * TURNS + j + 1)
                    nc.vector.tensor_copy(probs_t[:, j * GROUP:(j + 1) * GROUP, :].rearrange("p a b -> p (a b)"),
                                          ps_d[j % BANKS][:]).then_inc(d_turned_kept[1], 1)
                dve.wait_ge(d_probs_made, k + 1)
                nc.vector.reciprocal(inv_sum_d[:], row_sum[:]).then_inc(d_inv_sum, 1)

            def dense_pack(k):
                dve.wait_ge(d_inv_sum, k + 1)
                dve.wait_ge(d_out_ready, k + 1)
                if not is_early(k, 1):
                    dve.wait_ge(d_unpacked, k)
                nc.vector.scalar_tensor_tensor(packed, ps_o[:, 0:D].rearrange("p (h d) -> p h d", d=HD),
                                               inv_sum_d[:], pack_mask[:].unsqueeze(2).broadcast_to([P, HEADS, HD]),
                                               ALU.mult, ALU.mult).then_inc(d_packed, 1)

            def dense_finish(k):
                dve.wait_ge(d_unpacked, k + 1)
                nc.vector.tensor_copy(attn_d[:], ps_a[:, 0:D]).then_inc(d_attn_made, 1)

            def search(s, q):
                candidates(s)
                candidates_int(s)
                spread_folds(s)
                note_candidates(s)
                rounds = kind_of(s).rounds
                for r in range(rounds):
                    find_round(s, r)
                    if r + 1 < rounds:
                        take_round(s, r)
                decode_bias(s, q)
                decode_low(s)
                decode_column(s)
                decode_index(s, q)
                note_found(s)

            search(0, 0)
            dense_mask(0)
            mark(1, 1, 0)
            for b in range(2):
                dve.wait_ge(q_stored[b], 16 * (GROUPS // 2))
            dve.wait_ge(d_bias_made, 1)
            dve.wait_ge(d_q_kept, 1)
            dense_scores(0, 0, True)
            search(1, 1)
            mark(2, 0, 1)
            for b in range(2):
                dve.wait_ge(kv_stored[b], 16 * (GROUPS // 2))
            dve.wait_ge(p_values_kept, GROUPS)
            dense_keep(0)
            search(2, 2)

            def step(s, b, r, i, q):
                c, cq = s + SEEK, (q + SEEK) % DEPTH
                tail = not is_early(s, 1)
                ahead = there(s, SEEK) and not is_early(s, 1)
                rounds = kind_of(c).rounds if ahead else 0
                if not is_early(s, 2):
                    tail_rstd(s - 2)
                if ahead:
                    candidates(c)
                if not is_early(s, 2):
                    tail_norm(s - 2, b)
                if ahead:
                    candidates_int(c)
                if there(s, 3):
                    mark(s + 3, 1 - b, r + 1 + b)
                if ahead:
                    spread_folds(c)
                    note_candidates(c)
                    find_round(c, 0)
                if not is_early(s, 3):
                    tail_end(s - 3, 1 - b)
                for n in range(1, rounds):
                    take_round(c, n - 1)
                    find_round(c, n)
                if tail:
                    finish_attention(s - 1)
                if ahead:
                    decode_bias(c, cq)
                products(s, b, r, i, q)
                if ahead:
                    decode_low(c)
                scores_of_slots(s)
                if ahead:
                    decode_column(c)
                mask_slots(s, q)
                if ahead:
                    decode_index(c, cq)
                max_slots(s)
                if ahead:
                    note_found(c)
                subtract_max(s)
                if tail:
                    tail_residual(s - 1, 1 - b)
                    tail_stat6(s - 1, 1 - b)
                    tail_stats(s - 1)
                weigh_values(s, b, q)
                if is_early(s, 1):
                    dense_pack(0)
                    dense_finish(0)

            def whole_tail(n, b):
                tail_residual(n, b)
                tail_stat6(n, b)
                tail_stats(n)
                tail_rstd(n)
                tail_norm(n, b)
                tail_end(n, b)

            steady(dve, step)
            tail_rstd(TILES - 2)
            tail_norm(TILES - 2, 0)
            tail_end(TILES - 3, 1)
            finish_attention(TILES - 1)
            tail_residual(TILES - 1, 1)
            tail_stat6(TILES - 1, 1)
            tail_stats(TILES - 1)
            tail_rstd(TILES - 1)
            tail_norm(TILES - 1, 1)
            dve.wait_ge(worst_step, 2 * (TILES + 1))
            nc.vector.tensor_reduce(worst[:, 0:1], worst_cand[:], AX.X, ALU.max).then_inc(worst_step, 1)
            nc.vector.tensor_copy(worst[:, 1:2], worst_found[:]).then_inc(worst_step, 1)
            dve.wait_ge(worst_step, 2 * (TILES + 2))
            nc.vector.tensor_scalar(worst[:], worst[:], float(BANK), None, ALU.is_ge).then_inc(worst_step, 1)
            dve.wait_ge(worst_step, 2 * (TILES + 2) + 1)
            nc.vector.tensor_reduce(too_many[:], worst[:], AX.X, ALU.max).then_inc(flag_summed, 1)
            dve.wait_ge(flag_summed, 2)
            nc.vector.tensor_copy(dense_needed[:], ps_c[0:1, 0:1]).then_inc(flag_made, 1)
            tail_end(TILES - 2, 0)
            tail_end(TILES - 1, 1)

            dve.wait_ge(flag_made, 1)
            with dve.If(dve.value_load(dense_needed[0:1, 0:1], min_val=0, max_val=P) > 0):
                with dve.Fori(0, TILES) as t:
                    dve.wait_ge(d_q_kept, t + 2)
                    for i in range(PARTS_OF_TILE):
                        k = t * PARTS_OF_TILE + (i + 1)
                        dense_mask(k)
                        dve.wait_ge(d_bias_made, t * PARTS_OF_TILE + (i + 2))
                        dense_scores(k, i)
                        dense_keep(k)
                        dense_pack(k)
                    dense_finish(t * PARTS_OF_TILE + PARTS_OF_TILE)
                    whole_tail(TILES + t, 0)


NAMES = ["x", "adj"] + [f"L0_gnn_{n}" for n in
                        ("w_qkv", "w_proj", "b_proj", "w1", "b1", "w2", "b2", "g1", "be1", "g2", "be2")]


def kernel(**inputs):
    import numpy as np
    import concourse.bacc as bacc
    from concourse.bass_utils import run_bass_kernel_spmd

    nc = bacc.Bacc("TRN2", target_bir_lowering=False, num_devices=1)
    arrays, args = {}, []
    for name in NAMES:
        a = np.ascontiguousarray(inputs[name])
        arrays[f"in_{name}"] = a
        args.append(nc.dram_tensor(f"in_{name}", a.shape, mybir.dt.from_np(a.dtype), kind="ExternalInput").ap())
    out = nc.dram_tensor("out_0", inputs["x"].shape, F32, kind="ExternalOutput").ap()
    graph_layer(nc, *args, out)
    result = run_bass_kernel_spmd(nc, [arrays], core_ids=[0])
    return result.results[0]["out_0"]
```
